# Optimizing a Trainium2 kernel written in Bass

```python
import numpy as np
import jax
import jax.numpy as jnp

def _softmax(x, axis=-1):
    return jax.nn.softmax(x, axis=axis)

def _gelu(x):
    return jax.nn.gelu(x, approximate=True)

def _silu(x):
    return jax.nn.silu(x)

def _sigmoid(x):
    return jax.nn.sigmoid(x)

def _layernorm(x, axis=-1, eps=1e-05):
    m = jnp.mean(x, axis=axis, keepdims=True)
    v = jnp.var(x, axis=axis, keepdims=True)
    return (x - m) / jnp.sqrt(v + eps)

def _scatter_add(tgt, idx, src, axis=0):
    return tgt.at[idx].add(src)

def _segment_sum(src, seg, n):
    return jax.ops.segment_sum(src, seg, n)
kernel_name = 'mk_dlrm_tower_d1_rec_r8_e28dc5'

def setup_inputs(seed: int=0):
    np.random.seed(seed)
    _w = jnp.asarray

    def _rec_inputs():
        import jax
        import jax.numpy as jnp
        _tk = jax.random.key(seed)
        dense_ctx = jax.random.normal(jax.random.fold_in(_tk, 190), (512, 16), jnp.float32)
        ids = jnp.stack([jax.random.randint(jax.random.fold_in(_tk, 200 + f), (512,), 0, v, jnp.int32) for f, v in enumerate([125000, 12500, 125000, 125000, 1250, 125000, 125000, 12500, 1250, 125000, 1000, 1250, 1250, 1250, 12500, 12500, 12500, 1250, 1000, 12500, 1000, 1250, 125000, 125000, 1000, 1000, 1000, 12500, 1000, 12500, 1250, 1000, 125000, 1000, 1250, 12500, 125000, 1250, 1000])], axis=1)
        tbl_0 = 0.05 * jax.random.normal(jax.random.fold_in(_tk, 500 + 0), (125000, 16), jnp.float32)
        tbl_1 = 0.05 * jax.random.normal(jax.random.fold_in(_tk, 500 + 1), (12500, 16), jnp.float32)
        tbl_2 = 0.05 * jax.random.normal(jax.random.fold_in(_tk, 500 + 2), (125000, 16), jnp.float32)
        tbl_3 = 0.05 * jax.random.normal(jax.random.fold_in(_tk, 500 + 3), (125000, 16), jnp.float32)
        tbl_4 = 0.05 * jax.random.normal(jax.random.fold_in(_tk, 500 + 4), (1250, 16), jnp.float32)
        tbl_5 = 0.05 * jax.random.normal(jax.random.fold_in(_tk, 500 + 5), (125000, 16), jnp.float32)
        tbl_6 = 0.05 * jax.random.normal(jax.random.fold_in(_tk, 500 + 6), (125000, 16), jnp.float32)
        tbl_7 = 0.05 * jax.random.normal(jax.random.fold_in(_tk, 500 + 7), (12500, 16), jnp.float32)
        tbl_8 = 0.05 * jax.random.normal(jax.random.fold_in(_tk, 500 + 8), (1250, 16), jnp.float32)
        tbl_9 = 0.05 * jax.random.normal(jax.random.fold_in(_tk, 500 + 9), (125000, 16), jnp.float32)
        tbl_10 = 0.05 * jax.random.normal(jax.random.fold_in(_tk, 500 + 10), (1000, 16), jnp.float32)
        tbl_11 = 0.05 * jax.random.normal(jax.random.fold_in(_tk, 500 + 11), (1250, 16), jnp.float32)
        tbl_12 = 0.05 * jax.random.normal(jax.random.fold_in(_tk, 500 + 12), (1250, 16), jnp.float32)
        tbl_13 = 0.05 * jax.random.normal(jax.random.fold_in(_tk, 500 + 13), (1250, 16), jnp.float32)
        tbl_14 = 0.05 * jax.random.normal(jax.random.fold_in(_tk, 500 + 14), (12500, 16), jnp.float32)
        tbl_15 = 0.05 * jax.random.normal(jax.random.fold_in(_tk, 500 + 15), (12500, 16), jnp.float32)
        tbl_16 = 0.05 * jax.random.normal(jax.random.fold_in(_tk, 500 + 16), (12500, 16), jnp.float32)
        tbl_17 = 0.05 * jax.random.normal(jax.random.fold_in(_tk, 500 + 17), (1250, 16), jnp.float32)
        tbl_18 = 0.05 * jax.random.normal(jax.random.fold_in(_tk, 500 + 18), (1000, 16), jnp.float32)
        tbl_19 = 0.05 * jax.random.normal(jax.random.fold_in(_tk, 500 + 19), (12500, 16), jnp.float32)
        tbl_20 = 0.05 * jax.random.normal(jax.random.fold_in(_tk, 500 + 20), (1000, 16), jnp.float32)
        tbl_21 = 0.05 * jax.random.normal(jax.random.fold_in(_tk, 500 + 21), (1250, 16), jnp.float32)
        tbl_22 = 0.05 * jax.random.normal(jax.random.fold_in(_tk, 500 + 22), (125000, 16), jnp.float32)
        tbl_23 = 0.05 * jax.random.normal(jax.random.fold_in(_tk, 500 + 23), (125000, 16), jnp.float32)
        tbl_24 = 0.05 * jax.random.normal(jax.random.fold_in(_tk, 500 + 24), (1000, 16), jnp.float32)
        tbl_25 = 0.05 * jax.random.normal(jax.random.fold_in(_tk, 500 + 25), (1000, 16), jnp.float32)
        tbl_26 = 0.05 * jax.random.normal(jax.random.fold_in(_tk, 500 + 26), (1000, 16), jnp.float32)
        tbl_27 = 0.05 * jax.random.normal(jax.random.fold_in(_tk, 500 + 27), (12500, 16), jnp.float32)
        tbl_28 = 0.05 * jax.random.normal(jax.random.fold_in(_tk, 500 + 28), (1000, 16), jnp.float32)
        tbl_29 = 0.05 * jax.random.normal(jax.random.fold_in(_tk, 500 + 29), (12500, 16), jnp.float32)
        tbl_30 = 0.05 * jax.random.normal(jax.random.fold_in(_tk, 500 + 30), (1250, 16), jnp.float32)
        tbl_31 = 0.05 * jax.random.normal(jax.random.fold_in(_tk, 500 + 31), (1000, 16), jnp.float32)
        tbl_32 = 0.05 * jax.random.normal(jax.random.fold_in(_tk, 500 + 32), (125000, 16), jnp.float32)
        tbl_33 = 0.05 * jax.random.normal(jax.random.fold_in(_tk, 500 + 33), (1000, 16), jnp.float32)
        tbl_34 = 0.05 * jax.random.normal(jax.random.fold_in(_tk, 500 + 34), (1250, 16), jnp.float32)
        tbl_35 = 0.05 * jax.random.normal(jax.random.fold_in(_tk, 500 + 35), (12500, 16), jnp.float32)
        tbl_36 = 0.05 * jax.random.normal(jax.random.fold_in(_tk, 500 + 36), (125000, 16), jnp.float32)
        tbl_37 = 0.05 * jax.random.normal(jax.random.fold_in(_tk, 500 + 37), (1250, 16), jnp.float32)
        tbl_38 = 0.05 * jax.random.normal(jax.random.fold_in(_tk, 500 + 38), (1000, 16), jnp.float32)
        _rk = jax.random.fold_in(_tk, 7)
        W_top1 = 0.05 * jax.random.normal(jax.random.fold_in(_tk, 801), (400, 512), jnp.float32)
        W_top2 = 0.0441942 * jax.random.normal(jax.random.fold_in(_tk, 802), (512, 256), jnp.float32)
        W_top3 = 0.0625 * jax.random.normal(jax.random.fold_in(_tk, 803), (256, 1), jnp.float32)
        b_top1 = jnp.zeros((512,), jnp.float32)
        b_top2 = jnp.zeros((256,), jnp.float32)
        return (dense_ctx, ids, tbl_0, tbl_1, tbl_2, tbl_3, tbl_4, tbl_5, tbl_6, tbl_7, tbl_8, tbl_9, tbl_10, tbl_11, tbl_12, tbl_13, tbl_14, tbl_15, tbl_16, tbl_17, tbl_18, tbl_19, tbl_20, tbl_21, tbl_22, tbl_23, tbl_24, tbl_25, tbl_26, tbl_27, tbl_28, tbl_29, tbl_30, tbl_31, tbl_32, tbl_33, tbl_34, tbl_35, tbl_36, tbl_37, tbl_38, W_top1, b_top1, W_top2, b_top2, W_top3)
    dense_ctx, ids, tbl_0, tbl_1, tbl_2, tbl_3, tbl_4, tbl_5, tbl_6, tbl_7, tbl_8, tbl_9, tbl_10, tbl_11, tbl_12, tbl_13, tbl_14, tbl_15, tbl_16, tbl_17, tbl_18, tbl_19, tbl_20, tbl_21, tbl_22, tbl_23, tbl_24, tbl_25, tbl_26, tbl_27, tbl_28, tbl_29, tbl_30, tbl_31, tbl_32, tbl_33, tbl_34, tbl_35, tbl_36, tbl_37, tbl_38, W_top1, b_top1, W_top2, b_top2, W_top3 = _rec_inputs()

    def _L0_rec_setup():
        import jax, jax.numpy as jnp
        import numpy as np
        B, F0, D = (512, 39, 16)
        CIN = [128, 128, 128]

        def _cin_layer(X0, Xi, W, b):
            H = W.shape[0]
            F0_, Fi = (X0.shape[1], Xi.shape[1])
            Wr = W.reshape(H, F0_, Fi)
            return jnp.einsum('hjk,bjd,bkd->bhd', Wr, X0, Xi) + b[None, :, None]
        key = jax.random.key(seed)
        ks = jax.random.split(key, 4)
        x = jax.random.normal(ks[0], (B, F0, D), dtype=jnp.float32)
        fields = [F0] + CIN
        inp = {'embedded_features': x}
        for i in range(len(CIN)):
            cin = F0 * fields[i]
            cout = fields[i + 1]
            kw = jax.random.fold_in(ks[1], i)
            inp[f'W{i}'] = jax.random.normal(kw, (cout, cin), dtype=jnp.float32) / np.sqrt(cin)
            inp[f'b{i}'] = jnp.zeros((cout,), dtype=jnp.float32)
        return inp
    _L0_rec_all = _L0_rec_setup()
    _L0_rec_in = {k: v for k, v in _L0_rec_all.items() if k in ('W0', 'b0', 'W1', 'b1', 'W2', 'b2')}
    del _L0_rec_all
    return {'dense_ctx': dense_ctx, 'ids': ids, 'tbl_0': tbl_0, 'tbl_1': tbl_1, 'tbl_2': tbl_2, 'tbl_3': tbl_3, 'tbl_4': tbl_4, 'tbl_5': tbl_5, 'tbl_6': tbl_6, 'tbl_7': tbl_7, 'tbl_8': tbl_8, 'tbl_9': tbl_9, 'tbl_10': tbl_10, 'tbl_11': tbl_11, 'tbl_12': tbl_12, 'tbl_13': tbl_13, 'tbl_14': tbl_14, 'tbl_15': tbl_15, 'tbl_16': tbl_16, 'tbl_17': tbl_17, 'tbl_18': tbl_18, 'tbl_19': tbl_19, 'tbl_20': tbl_20, 'tbl_21': tbl_21, 'tbl_22': tbl_22, 'tbl_23': tbl_23, 'tbl_24': tbl_24, 'tbl_25': tbl_25, 'tbl_26': tbl_26, 'tbl_27': tbl_27, 'tbl_28': tbl_28, 'tbl_29': tbl_29, 'tbl_30': tbl_30, 'tbl_31': tbl_31, 'tbl_32': tbl_32, 'tbl_33': tbl_33, 'tbl_34': tbl_34, 'tbl_35': tbl_35, 'tbl_36': tbl_36, 'tbl_37': tbl_37, 'tbl_38': tbl_38, 'W_top1': W_top1, 'b_top1': b_top1, 'W_top2': W_top2, 'b_top2': b_top2, 'W_top3': W_top3, 'L0_rec_W0': _L0_rec_in['W0'], 'L0_rec_b0': _L0_rec_in['b0'], 'L0_rec_W1': _L0_rec_in['W1'], 'L0_rec_b1': _L0_rec_in['b1'], 'L0_rec_W2': _L0_rec_in['W2'], 'L0_rec_b2': _L0_rec_in['b2']}

def reference(dense_ctx, ids, tbl_0, tbl_1, tbl_2, tbl_3, tbl_4, tbl_5, tbl_6, tbl_7, tbl_8, tbl_9, tbl_10, tbl_11, tbl_12, tbl_13, tbl_14, tbl_15, tbl_16, tbl_17, tbl_18, tbl_19, tbl_20, tbl_21, tbl_22, tbl_23, tbl_24, tbl_25, tbl_26, tbl_27, tbl_28, tbl_29, tbl_30, tbl_31, tbl_32, tbl_33, tbl_34, tbl_35, tbl_36, tbl_37, tbl_38, W_top1, b_top1, W_top2, b_top2, W_top3, L0_rec_W0, L0_rec_b0, L0_rec_W1, L0_rec_b1, L0_rec_W2, L0_rec_b2):
    import jax
    import jax.numpy as jnp

    def _L0_rec_ref(embedded_features, W0, b0, W1, b1, W2, b2):
        import jax, jax.numpy as jnp
        import numpy as np
        B, F0, D = (512, 39, 16)
        CIN = [128, 128, 128]

        def _cin_layer(X0, Xi, W, b):
            H = W.shape[0]
            F0_, Fi = (X0.shape[1], Xi.shape[1])
            Wr = W.reshape(H, F0_, Fi)
            return jnp.einsum('hjk,bjd,bkd->bhd', Wr, X0, Xi) + b[None, :, None]
        X0 = embedded_features
        Ws = [(W0, b0), (W1, b1), (W2, b2)]
        Xi = X0
        res = []
        for W, b in Ws:
            Xi = _cin_layer(X0, Xi, W, b)
            res.append(Xi.sum(axis=2))
        return jnp.concatenate(res, axis=1)
    e = jnp.stack([tbl_0[ids[:, 0]], tbl_1[ids[:, 1]], tbl_2[ids[:, 2]], tbl_3[ids[:, 3]], tbl_4[ids[:, 4]], tbl_5[ids[:, 5]], tbl_6[ids[:, 6]], tbl_7[ids[:, 7]], tbl_8[ids[:, 8]], tbl_9[ids[:, 9]], tbl_10[ids[:, 10]], tbl_11[ids[:, 11]], tbl_12[ids[:, 12]], tbl_13[ids[:, 13]], tbl_14[ids[:, 14]], tbl_15[ids[:, 15]], tbl_16[ids[:, 16]], tbl_17[ids[:, 17]], tbl_18[ids[:, 18]], tbl_19[ids[:, 19]], tbl_20[ids[:, 20]], tbl_21[ids[:, 21]], tbl_22[ids[:, 22]], tbl_23[ids[:, 23]], tbl_24[ids[:, 24]], tbl_25[ids[:, 25]], tbl_26[ids[:, 26]], tbl_27[ids[:, 27]], tbl_28[ids[:, 28]], tbl_29[ids[:, 29]], tbl_30[ids[:, 30]], tbl_31[ids[:, 31]], tbl_32[ids[:, 32]], tbl_33[ids[:, 33]], tbl_34[ids[:, 34]], tbl_35[ids[:, 35]], tbl_36[ids[:, 36]], tbl_37[ids[:, 37]], tbl_38[ids[:, 38]]], axis=1)
    z = _L0_rec_ref(e, L0_rec_W0, L0_rec_b0, L0_rec_W1, L0_rec_b1, L0_rec_W2, L0_rec_b2)
    z = z.reshape(z.shape[0], -1)
    h = jnp.concatenate([z, dense_ctx], axis=1)
    h = jnp.maximum(h @ W_top1 + b_top1, 0.0)
    h = jnp.maximum(h @ W_top2 + b_top2, 0.0)
    y = h @ W_top3
    return y

_drawn_inputs = setup_inputs


def setup_inputs(seed=0):
    import zlib

    import numpy as np

    out = dict(_drawn_inputs(seed))
    spreads = {'b_top1': (0.0, 0.1),
     'b_top2': (0.0, 0.1),
     'L0_rec_b0': (0.0, 0.1),
     'L0_rec_b1': (0.0, 0.1),
     'L0_rec_b2': (0.0, 0.1)}
    factors = {'tbl_0': 8.0,
     'tbl_1': 6.03,
     'tbl_2': 5.377,
     'tbl_3': 7.444,
     'tbl_4': 8.0,
     'tbl_5': 8.0,
     'tbl_6': 8.0,
     'tbl_7': 7.027,
     'tbl_8': 8.0,
     'tbl_9': 8.0,
     'tbl_10': 8.0,
     'tbl_11': 6.858,
     'tbl_12': 8.0,
     'tbl_13': 8.0,
     'tbl_14': 4.215,
     'tbl_15': 5.395,
     'tbl_16': 8.0,
     'tbl_17': 8.0,
     'tbl_18': 8.0,
     'tbl_19': 6.126,
     'tbl_20': 7.222,
     'tbl_21': 8.0,
     'tbl_22': 8.0,
     'tbl_23': 8.0,
     'tbl_24': 8.0,
     'tbl_25': 7.418,
     'tbl_26': 5.772,
     'tbl_27': 8.0,
     'tbl_28': 8.0,
     'tbl_29': 8.0,
     'tbl_30': 6.751,
     'tbl_31': 6.242,
     'tbl_32': 8.0,
     'tbl_33': 6.251,
     'tbl_34': 8.0,
     'tbl_35': 6.639,
     'tbl_36': 8.0,
     'tbl_37': 6.526,
     'tbl_38': 8.0,
     'L0_rec_W0': 3.17}
    for name, (base, spread) in spreads.items():
        noise = np.random.default_rng([zlib.crc32(name.encode()), seed]).standard_normal(out[name].shape)
        drawn = base * np.exp(spread * noise) if base else spread * noise
        out[name] = jnp.asarray(drawn.astype(out[name].dtype))
    for name, factor in factors.items():
        out[name] = (out[name] * factor).astype(out[name].dtype)
    return out
```

```python
from contextlib import ExitStack

import numpy as np

import concourse.bass as bass
from concourse import mybir

F32 = mybir.dt.float32
F32R = mybir.dt.float32r
BF16 = mybir.dt.bfloat16
I32 = mybir.dt.int32
ALU = mybir.AluOpType
ACT = mybir.ActivationFunctionType
AX = mybir.AxisListType

BATCH, FIELDS, DIM, HID = 512, 39, 16, 128
P = 128
TILE = 512
ROWS = TILE // DIM
STEPS = BATCH // ROWS
BLOCKS = BATCH // P
PER_BLOCK = STEPS // BLOCKS
PARTS = 3
STACK = PARTS * FIELDS
L0_TILES = 7
J_GROUP, K_GROUP = 8, 16
A_GROUPS = -(-FIELDS // J_GROUP)
B_GROUPS = HID // K_GROUP
PAIRS = A_GROUPS * B_GROUPS // 2
A_PAIRS = B_GROUPS // 2
RING, RING_LOW = 4, 2
SUB = TILE // P
SUB_ROWS = P // DIM
QUART = DIM // 4
TOP1, TOP2 = 512, 256
L2_ROWS = 2 * ROWS
DMA_INC = 16
CONSTANTS = 7
SEL0, SELA = (L0_TILES + 1) * STACK, A_GROUPS * P
SEL_COLUMNS = SEL0 + SELA + FIELDS


def pool_doubles(block):
    return 14 if block == BLOCKS - 1 else 11


def takers(first_step, last_block):
    n = 0 if first_step else pool_doubles(BLOCKS - 1 if last_block else 0)
    return ["pool" if (i + 1) * n // PAIRS > i * n // PAIRS else "dve" for i in range(PAIRS)]


def build(nc, ids, tables, dense, w0a, w0b, w1, w2, wt1, wt2, wt3, bias, bt1, bt2, selections, mask, eye, out):
    ctx = ExitStack()
    with ctx:
        def sb(name, shape, dt=F32):
            return ctx.enter_context(nc.sbuf_tensor(name, shape, dt))

        def sem(name):
            return ctx.enter_context(nc.semaphore(name))

        idx = sb("idx", [P, BLOCKS, FIELDS], I32)
        emb = sb("emb", [P, 2, FIELDS * DIM])
        parts = sb("parts", [STACK, BATCH * DIM], BF16)
        w1_high = sb("w1_high", [P, A_GROUPS * B_GROUPS, HID], F32R)
        w1_low = sb("w1_low", [P, A_GROUPS * B_GROUPS, HID], F32R)
        w0_sb = sb("w0_sb", [STACK, L0_TILES, HID])
        w2_sb = sb("w2_sb", [P, FIELDS, HID])
        Z = sb("Z", [P, RING, 2 * TILE])
        Z_high = sb("Z_high", [P, RING, 2 * TILE], F32R)
        Z_low = sb("Z_low", [P, RING_LOW, 2 * TILE], F32R)
        z0 = sb("z0", [STACK, 2, TILE])
        x0_rep = sb("x0_rep", [STACK, TILE])
        x1 = sb("x1", [P, 2, TILE])
        x2 = sb("x2", [P, 2, TILE])
        x2T = sb("x2T", [P, SUB, P])
        x0_diag = sb("x0_diag", [P, SUB, SUB_ROWS, FIELDS])
        G = sb("G", [P, FIELDS, L2_ROWS])
        res = sb("res", [P, 3, BATCH])
        dense_sb = sb("dense_sb", [DIM, BATCH])
        stage = sb("stage", [P, QUART, PARTS, FIELDS])
        part_high = sb("part_high", [STACK, P, QUART], BF16)
        part_mid = sb("part_mid", [STACK, P, QUART], BF16)
        rest = sb("rest", [STACK, P, QUART])
        sel_sb = sb("sel_sb", [STACK, SEL_COLUMNS], BF16)
        sel0_sb = sel_sb[:, 0:SEL0].rearrange("p (t m) -> p t m", m=STACK)
        selA_sb = sel_sb[:, SEL0:SEL0 + SELA].rearrange("p (a m) -> p a m", m=P)
        selT_sb = sel_sb[:, SEL0 + SELA:SEL_COLUMNS]
        mask_sb = sb("mask_sb", [P, SUB_ROWS])
        eye_sb = sb("eye_sb", [P, P])
        bias_sb = sb("bias_sb", [P, 4])
        bt1_sb = sb("bt1_sb", [P, TOP1 // P])
        bt2_sb = sb("bt2_sb", [P, TOP2 // P])
        wt3_sb = sb("wt3_sb", [P, TOP2 // P])
        y_sb = sb("y_sb", [1, BATCH])
        with nc.sbuf_tensor("x1_rep", [P, 2, B_GROUPS, TILE], F32) as x1_rep:
            pass
        wt1_sb = sb("wt1_sb", [P, 4, TOP1])
        wt2_sb = sb("wt2_sb", [P, TOP1 // P, TOP2])
        h1 = sb("h1", [P, TOP1 // P, BATCH])
        h2 = sb("h2", [P, TOP2 // P, BATCH])
        w1_stage = x1_rep[:].rearrange("p a b c -> p (a b c)")[:, 0:A_GROUPS * B_GROUPS * HID]
        sel_stage = Z[:].rearrange("p a b -> p (a b)")[0:STACK, 0:SEL_COLUMNS]
        w0b_stage = G[:].rearrange("p j b -> p (j b)")[0:STACK, 0:L0_TILES * HID]

        bank = [ctx.enter_context(nc.psum_tensor(f"bank{i}", [P, TILE], F32)) for i in range(8)]
        bank_a, bank_s, bank_x1, bank_x2, bank_r2 = bank[0:2], bank[2:4], bank[4], [bank[5], bank[7]], bank[6]
        bank_h1 = [bank[0], bank[1], bank[4], bank[5]]

        idx_in, w1_in, w0_in, w0b_in, w2_in = (sem(n) for n in ("idx_in", "w1_in", "w0_in", "w0b_in", "w2_in"))
        const_in, dense_in, top_in, y_out = (sem(n) for n in ("const_in", "dense_in", "top_in", "y_out"))
        gathered = [sem("gathered0"), sem("gathered1")] + [sem("gathered_later")] * (BLOCKS - 2)
        w1_high_ready, w1_low_ready, w0_ready, bias_ready, sel_ready = (
            sem(n) for n in ("w1_high_ready", "w1_low_ready", "w0_ready", "bias_ready", "sel_ready"))
        stage_ready = sem("stage_ready")
        turned = sem("turned")
        high_ready = sem("high_ready")
        rest_ready = sem("rest_ready")
        mid_ready = sem("mid_ready")
        low_ready = sem("low_ready")
        mid_stacked = sem("mid_stacked")
        parts_ready = sem("parts_ready")
        l0_spread = sem("l0_spread")
        x0_rep_ready = sem("x0_rep_ready")
        z0_ready = sem("z0_ready")
        l0_done = sem("l0_done")
        x1_ready = sem("x1_ready")
        x1_spread = [sem(f"x1_spread{i}") for i in range(2)]
        x1_pooled = sem("x1_pooled")
        a_ready = sem("a_ready")
        z_ready = sem("z_ready")
        z_high_ready = sem("z_high_ready")
        z_low_dve = sem("z_low_dve")
        z_low_pool = sem("z_low_pool")
        used = sem("used")
        x2_ready = sem("x2_ready")
        x2_pooled = sem("x2_pooled")
        x0_turned = sem("x0_turned")
        x2_turned = sem("x2_turned")
        diag_ready = sem("diag_ready")
        x2T_ready = sem("x2T_ready")
        g_done = sem("g_done")
        g_ready = sem("g_ready")
        l2_done = sem("l2_done")
        res2_ready = sem("res2_ready")
        h1_done, h1_ready, h2_done, h2_ready, y_done, y_ready = (
            sem(n) for n in ("h1_done", "h1_ready", "h2_done", "h2_ready", "y_done", "y_ready"))

        def wait(eng, semaphore, value):
            if not isinstance(value, int) or value > 0:
                eng.wait_ge(semaphore, value)

        def part_wait(eng):
            eng.wait_ge(const_in, CONSTANTS * DMA_INC)

        def taker(blk, q, i):
            return takers(isinstance(blk, int) and blk == 0 and q == 0, isinstance(blk, int) and blk == BLOCKS - 1)[i]

        def low_count(who, blk, q, i):
            if not isinstance(blk, int):
                per_block = low_count(who, 2, 0, -1) - low_count(who, 1, 0, -1)
                return (blk - 1) * per_block + low_count_in(who, 1, q, i)
            return low_count_in(who, blk, q, i)

        def low_count_in(who, blk, q, i):
            n = 0
            for step in range(PER_BLOCK * blk + q + 1):
                kinds = takers(step == 0, step // PER_BLOCK == BLOCKS - 1)
                n += sum(k == who for k in (kinds if step < PER_BLOCK * blk + q else kinds[:i + 1]))
            return n

        def before(blk, q, i, back):
            i -= back
            if i < 0:
                i, q = i + PAIRS, q - 1
            if q < 0:
                if isinstance(blk, int) and blk == 0:
                    return None
                q += PER_BLOCK
                blk = blk - 1
            return blk, q, i

        def wait_low(eng, blk, q, i):
            if isinstance(blk, int):
                who = takers(blk == 0 and q == 0, blk == BLOCKS - 1)[i]
            else:
                who = takers(False, False)[i]
            eng.wait_ge(z_low_pool if who == "pool" else z_low_dve, low_count(who, blk, q, i))

        def preps(blk, q):
            if q not in (1, 2) or (isinstance(blk, int) and blk == BLOCKS - 1):
                return []
            return [(2 * (q - 1) + c, 4 * (blk + 1) + 2 * (q - 1) + c) for c in range(2)]

        def has_next(blk, q):
            return not (isinstance(blk, int) and PER_BLOCK * blk + q == STEPS - 1)

        def is_step(blk, q, n):
            return isinstance(blk, int) and PER_BLOCK * blk + q == n

        def block_columns(blk):
            return parts[:, bass.ds(blk * (P * DIM), P * DIM)].rearrange("p (b d) -> p b d", d=DIM)

        block = ctx.enter_context(nc.Block())

        @block.sync
        def _(sp):
            sp.dma_start(idx[:], ids).then_inc(idx_in, DMA_INC)
            for dst, src in ((eye_sb[:], eye), (sel_stage, selections), (mask_sb[:], mask),
                             (bias_sb[:, 0:3], bias), (bt1_sb[:], bt1), (bt2_sb[:], bt2), (wt3_sb[:], wt3)):
                sp.dma_start(dst, src).then_inc(const_in, DMA_INC)
            sp.dma_start(w1_stage, w1).then_inc(w1_in, DMA_INC)
            sp.dma_start(w0_sb[:], w0a).then_inc(w0_in, DMA_INC)
            sp.dma_start(w0b_stage, w0b).then_inc(w0b_in, DMA_INC)
            sp.dma_start(dense_sb[:], dense).then_inc(dense_in, DMA_INC)
            sp.dma_start(w2_sb[:], w2).then_inc(w2_in, DMA_INC)
            sp.wait_ge(w1_high_ready, 1)
            sp.wait_ge(w1_low_ready, 1)

            def spread_x1(t, parity):
                sp.wait_ge(x1_ready, t + 1)
                for b in range(B_GROUPS):
                    rows = x1[K_GROUP * b:K_GROUP * (b + 1), parity, :]
                    sp.dma_start(x1_rep[:, parity, b, :],
                                 rows.unsqueeze(1).to_broadcast([K_GROUP, J_GROUP, TILE])
                                 ).then_inc(x1_spread[parity], DMA_INC)

            def steps(blk):
                for q in range(PER_BLOCK):
                    if has_next(blk, q):
                        spread_x1(PER_BLOCK * blk + q + 1, (q + 1) % 2)

            spread_x1(0, 0)
            steps(0)
            with sp.Fori(1, BLOCKS - 1) as blk:
                steps(blk)
            steps(BLOCKS - 1)
            sp.wait_ge(z_ready, PAIRS * STEPS)
            sp.dma_start(wt1_sb[:, 0:3, :], wt1[0:3 * P, :].rearrange("(c p) n -> p c n", p=P)).then_inc(top_in, DMA_INC)
            sp.dma_start(wt1_sb[0:DIM, 3, :], wt1[3 * P:3 * P + DIM, :]).then_inc(top_in, DMA_INC)
            sp.dma_start(wt2_sb[:], wt2.rearrange("(c p) n -> p c n", p=P)).then_inc(top_in, DMA_INC)
            sp.wait_ge(y_ready, 1)
            sp.dma_start(out.rearrange("b o -> o b"), y_sb[:]).then_inc(y_out, DMA_INC)
            sp.wait_ge(y_out, DMA_INC)

        @block.gpsimd
        def _(pool):
            def gather(blk, f):
                pool.indirect_dma_start(emb[:, blk % 2, f * DIM:(f + 1) * DIM], None, tables[f],
                                        bass.IndirectOffsetOnAxis(ap=idx[:, blk, f:f + 1], axis=0)
                                        ).then_inc(gathered[blk], DMA_INC)

            pool.wait_ge(idx_in, DMA_INC)
            todo = [(b, f) for b in range(2, BLOCKS) for f in range(FIELDS)]
            for b in range(2):
                for f in range(FIELDS):
                    gather(b, f)
            for step in range(STEPS):
                blk, q = divmod(step, PER_BLOCK)
                for i in range(PAIRS):
                    if taker(blk, q, i) == "pool":
                        pool.wait_ge(z_high_ready, PAIRS * step + i + 1)
                        wait(pool, used, PAIRS * step + i + 1 - RING_LOW)
                        pool.tensor_tensor(Z_low[:, i % RING_LOW, :], Z[:, i % RING, :],
                                           Z_high[:, i % RING, :].bitcast(F32), ALU.subtract).then_inc(z_low_pool, 1)
                    if step and i % 2 == 0 and todo:
                        b, f = todo.pop(0)
                        if f == 0:
                            pool.wait_ge(stage_ready, 4 * (b - 1))
                            wait(pool, gathered[b], (b - 2) * FIELDS * DMA_INC)
                        gather(b, f)

        @block.scalar
        def _(act):
            def copy(dst, src):
                return nc.scalar.copy(dst, src)

            def stage_quarter(rows, quarter, number):
                part_wait(act)
                wait(act, turned, number)
                src = rows.rearrange("p (f d) -> p d f", d=DIM)[:, QUART * quarter:QUART * (quarter + 1), :]
                copy(stage[:], src.unsqueeze(2).to_broadcast([P, QUART, PARTS, FIELDS])).then_inc(stage_ready, 1)

            def quarter_high(number, src):
                act.wait_ge(turned, number + 1)
                wait(act, parts_ready, number)
                copy(part_high[:], src[0:STACK, :].rearrange("p (d b) -> p b d", d=QUART)).then_inc(high_ready, 1)

            def quarter_mid(number):
                act.wait_ge(rest_ready, number + 1)
                copy(part_mid[:], rest[:]).then_inc(mid_ready, 1)

            def quarter_stack(blk, quarter, number):
                cols = block_columns(blk)[:, :, QUART * quarter:QUART * (quarter + 1)]
                part_wait(act)
                act.wait_ge(low_ready, number + 1)
                copy(cols[0:2 * FIELDS], part_mid[0:2 * FIELDS]).then_inc(mid_stacked, 1)
                part_wait(act)
                act.wait_ge(mid_stacked, number + 1)
                copy(cols[0:FIELDS], part_high[0:FIELDS]).then_inc(parts_ready, 1)

            def evacuate_x0_rep(t):
                act.wait_ge(l0_spread, (L0_TILES + 1) * t + 1)
                wait(act, z0_ready, L0_TILES * t)
                copy(x0_rep[:], bank_s[0][0:STACK, :]).then_inc(x0_rep_ready, 1)

            def evacuate_x1(t, parity, spreads):
                act.wait_ge(l0_done, L0_TILES * (t + 1))
                wait(act, x1_spread[parity], B_GROUPS * DMA_INC * spreads)
                wait(act, x1_pooled, t - 1)
                nc.scalar.activation(x1[:, parity, :], bank_x1[:], ACT.Identity, bias=bias_sb[:, 0:1]).then_inc(x1_ready, 1)

            def evacuate_x2(n, parity):
                act.wait_ge(used, PAIRS * n)
                wait(act, x2_turned, n - 2)
                wait(act, x2_pooled, n - 2)
                nc.scalar.activation(x2[:, parity, :], bank_x2[parity][:], ACT.Identity,
                                     bias=bias_sb[:, 1:2]).then_inc(x2_ready, 1)

            def evacuate_x2T(n):
                act.wait_ge(x2_turned, n)
                wait(act, g_done, SUB * (n - 1))
                copy(x2T[:].rearrange("p a b -> p (a b)"), bank_s[1][:]).then_inc(x2T_ready, 1)

            def evacuate_g(n, parity, sub, l2_before):
                act.wait_ge(g_done, SUB * (n - 1) + sub + 1)
                if parity == 0 and sub == 0:
                    wait(act, l2_done, l2_before)
                at = ROWS * parity + SUB_ROWS * sub
                copy(G[:, :, at:at + SUB_ROWS].rearrange("p j b -> p b j"),
                     bank_s[sub % 2][:, 0:SUB_ROWS * FIELDS].rearrange("p (b j) -> p b j", j=FIELDS)
                     ).then_inc(g_ready, 1)

            def evacuate_res2(number):
                part_wait(act)
                act.wait_ge(l2_done, number + 1)
                nc.scalar.activation(res[:, 2, bass.ds(number * L2_ROWS, L2_ROWS)], bank_r2[:, 0:L2_ROWS], ACT.Identity,
                                     bias=bias_sb[:, 3:4]).then_inc(res2_ready, 1)

            act.wait_ge(const_in, CONSTANTS * DMA_INC)
            nc.scalar.mul(bias_sb[:, 3:4], bias_sb[:, 2:3], float(DIM)).then_inc(bias_ready, 1)
            copy(sel_sb[:], sel_stage).then_inc(sel_ready, 1)
            act.wait_ge(w1_in, DMA_INC)
            copy(w1_high[:].rearrange("p t h -> p (t h)"), w1_stage).then_inc(w1_high_ready, 1)
            for m in range(4):
                if m == 0:
                    act.wait_ge(gathered[0], FIELDS * DMA_INC)
                stage_quarter(emb[:, 0, :], m, m)
                quarter_high(m, bank_s[m % 2])
                quarter_mid(m)
                quarter_stack(0, m, m)
            evacuate_x0_rep(0)
            evacuate_x1(0, 0, 0)
            act.wait_ge(bias_ready, 1)

            def steps(blk, next_rows=None, next_gathered=None, next_count=None):
                for q in range(PER_BLOCK):
                    n = PER_BLOCK * blk + q
                    t = n + 1
                    todo = preps(blk, q)
                    for i in range(PAIRS):
                        if i == 3 and not is_step(blk, q, 0):
                            evacuate_x2(n, (q - 1) % 2)
                        if i == 3 and has_next(blk, q):
                            evacuate_x0_rep(t)
                        if i == 9 and has_next(blk, q):
                            evacuate_x1(t, (q + 1) % 2, 2 * blk + (q + 1) // 2)
                        for c, (quarter, number) in enumerate(todo):
                            if i == (3, 9)[c]:
                                if quarter == 0:
                                    act.wait_ge(next_gathered, next_count)
                                stage_quarter(next_rows, quarter, number)
                            if i == (8, 12)[c]:
                                quarter_high(number, bank_s[c])
                            if i == (9, 13)[c]:
                                quarter_mid(number)
                            if i == (10, 15)[c]:
                                quarter_stack(blk + 1, quarter, number)
                        if not is_step(blk, q, 0):
                            if i == 14:
                                evacuate_x2T(n)
                            if q % 2 and i == 15 and not is_step(blk, q, 1):
                                evacuate_res2(2 * blk + (q - 3) // 2)
                            if i >= 16:
                                evacuate_g(n, (q - 1) % 2, i - 16, 2 * blk + (q - 1) // 2)
                        act.wait_ge(z_ready, PAIRS * n + i + 1)
                        wait(act, used, PAIRS * n + i + 1 - RING)
                        copy(Z_high[:, i % RING, :], Z[:, i % RING, :]).then_inc(z_high_ready, 1)

            steps(0, emb[:, 1, :], gathered[1], FIELDS * DMA_INC)
            emb_flat = emb[:].rearrange("p a b -> p (a b)")
            with act.Fori(1, BLOCKS - 1) as blk:
                steps(blk, emb_flat[:, bass.ds((blk - 1) * (FIELDS * DIM), FIELDS * DIM)],
                      gathered[2], blk * (FIELDS * DMA_INC))
            steps(BLOCKS - 1)

            n = STEPS
            evacuate_x2(n, (n - 1) % 2)
            evacuate_x2T(n)
            for sub in range(SUB):
                evacuate_g(n, (n - 1) % 2, sub, 0)
            evacuate_res2(STEPS // 2 - 1)
            for m in range(TOP1 // P):
                act.wait_ge(h1_done, m + 1)
                nc.scalar.activation(h1[:, m, :], bank_h1[m][:], ACT.Relu, bias=bt1_sb[:, m:m + 1]).then_inc(h1_ready, 1)
            for m in range(TOP2 // P):
                act.wait_ge(h2_done, m + 1)
                nc.scalar.activation(h2[:, m, :], bank_s[m][:], ACT.Relu, bias=bt2_sb[:, m:m + 1]).then_inc(h2_ready, 1)
            act.wait_ge(y_done, 1)
            copy(y_sb[:], bank_r2[0:1, :]).then_inc(y_ready, 1)

        @block.vector
        def _(dve):
            def quarter_rest(number, src):
                dve.wait_ge(high_ready, number + 1)
                wait(dve, low_ready, number)
                nc.vector.tensor_tensor(rest[:], src[0:STACK, :].rearrange("p (d b) -> p b d", d=QUART), part_high[:],
                                        ALU.subtract).then_inc(rest_ready, 1)

            def quarter_low(blk, quarter, number):
                cols = block_columns(blk)[:, :, QUART * quarter:QUART * (quarter + 1)]
                dve.wait_ge(mid_ready, number + 1)
                nc.vector.tensor_tensor(cols, rest[:], part_mid[:], ALU.subtract).then_inc(low_ready, 1)

            def l0_pairs(t, t_parity, k):
                if k == 0:
                    dve.wait_ge(x0_rep_ready, t + 1)
                dve.wait_ge(l0_spread, (L0_TILES + 1) * t + k + 2)
                wait(dve, l0_done, L0_TILES * t + k - 1)
                nc.vector.tensor_tensor(z0[:, (t_parity + k) % 2, :], bank_s[(k + 1) % 2][0:STACK, :], x0_rep[:],
                                        ALU.mult).then_inc(z0_ready, 1)

            def pool_x1(t, parity):
                part_wait(dve)
                dve.wait_ge(x1_ready, t + 1)
                nc.vector.reduce_sum(res[:, 0, bass.ds(t * ROWS, ROWS)],
                                     x1[:, parity, :].rearrange("p (b d) -> p b d", d=DIM), AX.X).then_inc(x1_pooled, 1)

            def pool_x2(n, parity):
                part_wait(dve)
                dve.wait_ge(x2_ready, n)
                nc.vector.reduce_sum(res[:, 1, bass.ds((n - 1) * ROWS, ROWS)],
                                     x2[:, parity, :].rearrange("p (b d) -> p b d", d=DIM), AX.X).then_inc(x2_pooled, 1)

            def diagonal(n):
                dve.wait_ge(x0_turned, n)
                wait(dve, g_done, SUB * (n - 1))
                x0_cols = bank_s[0][:, 0:SUB * FIELDS].rearrange("p (s j) -> p s j", j=FIELDS)
                nc.vector.tensor_tensor(
                    x0_diag[:], x0_cols.unsqueeze(2).to_broadcast([P, SUB, SUB_ROWS, FIELDS]),
                    mask_sb[:].unsqueeze(1).unsqueeze(3).to_broadcast([P, SUB, SUB_ROWS, FIELDS]),
                    ALU.mult).then_inc(diag_ready, 1)

            def low_part(at):
                blk, q, i = at
                n = PER_BLOCK * blk + q
                dve.wait_ge(z_high_ready, PAIRS * n + i + 1)
                wait(dve, used, PAIRS * n + i + 1 - RING_LOW)
                nc.vector.tensor_tensor(Z_low[:, i % RING_LOW, :], Z[:, i % RING, :], Z_high[:, i % RING, :].bitcast(F32),
                                        ALU.subtract).then_inc(z_low_dve, 1)

            dve.wait_ge(w0_in, DMA_INC)
            dve.wait_ge(w0b_in, DMA_INC)
            w0_flat = w0_sb[:].rearrange("p t h -> p (t h)")
            nc.vector.tensor_tensor(w0_flat, w0_flat, w0b_stage, ALU.add).then_inc(w0_ready, 1)
            dve.wait_ge(w1_high_ready, 1)
            nc.vector.tensor_tensor(w1_low[:].rearrange("p t h -> p (t h)"), w1_stage,
                                    w1_high[:].rearrange("p t h -> p (t h)").bitcast(F32), ALU.subtract).then_inc(w1_low_ready, 1)
            for m in range(4):
                quarter_rest(m, bank_s[m % 2])
                quarter_low(0, m, m)
            dve.wait_ge(const_in, CONSTANTS * DMA_INC)
            for k in range(L0_TILES):
                l0_pairs(0, 0, k)
            pool_x1(0, 0)

            def steps(blk):
                for q in range(PER_BLOCK):
                    n = PER_BLOCK * blk + q
                    t = n + 1
                    todo = preps(blk, q)
                    for i in range(PAIRS):
                        if has_next(blk, q):
                            for k in range(L0_TILES):
                                if i == 4 + k // 2:
                                    l0_pairs(t, (q + 1) % 2, k)
                            if i == 12:
                                pool_x1(t, (q + 1) % 2)
                        if not is_step(blk, q, 0):
                            if i == 8:
                                pool_x2(n, (q - 1) % 2)
                            if i == 13:
                                diagonal(n)
                        for c, (quarter, number) in enumerate(todo):
                            if i == (9, 13)[c]:
                                quarter_rest(number, bank_s[c])
                            if i == (10, 14)[c]:
                                quarter_low(blk + 1, quarter, number)
                        a, b = i // A_PAIRS, 2 * (i % A_PAIRS)
                        if i % A_PAIRS == 0:
                            dve.wait_ge(a_ready, A_GROUPS * n + a + 1)
                        if i == 0:
                            dve.wait_ge(x1_spread[q % 2], B_GROUPS * DMA_INC * (2 * blk + q // 2 + 1))
                        last_user = before(blk, q, i, RING)
                        if last_user is not None:
                            wait_low(dve, *last_user)
                        nc.vector.tensor_tensor(
                            Z[:, i % RING, :].rearrange("p (u c) -> p u c", u=2),
                            bank_a[(q + a) % 2][:].unsqueeze(1).to_broadcast([P, 2, TILE]),
                            x1_rep[:, q % 2, b:b + 2, :], ALU.mult).then_inc(z_ready, 1)
                        late = before(blk, q, i, 2)
                        if late is not None and taker_at(late) == "dve":
                            low_part(late)

            def taker_at(at):
                blk, q, i = at
                if isinstance(blk, int):
                    return takers(blk == 0 and q == 0, blk == BLOCKS - 1)[i]
                return takers(False, False)[i]

            steps(0)
            with dve.Fori(1, BLOCKS - 1) as blk:
                steps(blk)
            steps(BLOCKS - 1)
            for i in (PAIRS - 2, PAIRS - 1):
                if taker_at((BLOCKS - 1, PER_BLOCK - 1, i)) == "dve":
                    low_part((BLOCKS - 1, PER_BLOCK - 1, i))
            pool_x2(STEPS, (STEPS - 1) % 2)
            diagonal(STEPS)

        @block.tensor
        def _(pe):
            mm = nc.tensor.matmul

            def turn_quarter(number, dst):
                pe.wait_ge(stage_ready, number + 1)
                for d in range(QUART):
                    last = nc.tensor.transpose(dst[0:STACK, P * d:P * (d + 1)],
                                               stage[:, d].rearrange("p a f -> p (a f)"), eye_sb[:])
                last.then_inc(turned, 1)

            def l0_select(t, k):
                mm(bank_s[k % 2][0:STACK, :], sel0_sb[:, k, :], parts[:, bass.ds(t * TILE, TILE)],
                   start=True, stop=True).then_inc(l0_spread, 1)

            def l0_product(t, t_parity, k):
                pe.wait_ge(z0_ready, L0_TILES * t + k + 1)
                if k == 0:
                    wait(pe, x1_ready, t)
                mm(bank_x1[:], w0_sb[:, k, :], z0[:, (t_parity + k) % 2, :],
                   start=(k == 0), stop=(k == L0_TILES - 1)).then_inc(l0_done, 1)

            def select_fields(n, n_parity, a):
                mm(bank_a[(n_parity + a) % 2][:], selA_sb[:, a, :], parts[:, bass.ds(n * TILE, TILE)],
                   start=True, stop=True).then_inc(a_ready, 1)

            def high_products(n, q, i):
                pe.wait_ge(z_high_ready, PAIRS * n + i + 1)
                for u in range(2):
                    for w in (w1_high, w1_low):
                        mm(bank_x2[q % 2][:], w[:, 2 * i + u, :], Z_high[:, i % RING, u * TILE:(u + 1) * TILE],
                           start=(i == 0 and u == 0 and w is w1_high), stop=False)

            def low_products(at):
                blk, q, i = at
                wait_low(pe, blk, q, i)
                for u in range(2):
                    last = mm(bank_x2[q % 2][:], w1_high[:, 2 * i + u, :], Z_low[:, i % RING_LOW, u * TILE:(u + 1) * TILE],
                              start=False, stop=(i == PAIRS - 1 and u == 1))
                last.then_inc(used, 1)

            def turn_x0(n):
                for s in range(SUB):
                    last = mm(bank_s[0][:, s * FIELDS:(s + 1) * FIELDS], parts[:, bass.ds((n - 1) * TILE + s * P, P)],
                              selT_sb[:], start=True, stop=True)
                last.then_inc(x0_turned, 1)

            def turn_x2(n, parity):
                pe.wait_ge(x2_ready, n)
                for s in range(SUB):
                    last = nc.tensor.transpose(bank_s[1][:, s * P:(s + 1) * P], x2[:, parity, s * P:(s + 1) * P], eye_sb[:])
                last.then_inc(x2_turned, 1)

            def g_product(n, sub):
                if sub == 0:
                    pe.wait_ge(diag_ready, n)
                    pe.wait_ge(x2T_ready, n)
                if sub >= 2:
                    pe.wait_ge(g_ready, SUB * (n - 1) + sub - 1)
                mm(bank_s[sub % 2][:, 0:SUB_ROWS * FIELDS], x2T[:, sub, :],
                   x0_diag[:, sub].rearrange("p b j -> p (b j)"), start=True, stop=True).then_inc(g_done, 1)

            def l2_product(number, j):
                if j == 0:
                    pe.wait_ge(g_ready, 2 * SUB * (number + 1))
                    wait(pe, res2_ready, number)
                last = mm(bank_r2[:, 0:L2_ROWS], w2_sb[:, j, :], G[:, j, :], start=(j == 0), stop=(j == FIELDS - 1))
                if j == FIELDS - 1:
                    last.then_inc(l2_done, 1)

            pe.wait_ge(const_in, CONSTANTS * DMA_INC)
            for m in range(4):
                wait(pe, rest_ready, m - 1)
                turn_quarter(m, bank_s[m % 2])
            pe.wait_ge(parts_ready, 4)
            pe.wait_ge(sel_ready, 1)
            pe.wait_ge(w0_ready, 1)
            for k in range(L0_TILES + 1):
                if k >= 3:
                    pe.wait_ge(z0_ready, k - 2)
                elif k == 2:
                    pe.wait_ge(x0_rep_ready, 1)
                l0_select(0, k)
                if k >= 2:
                    l0_product(0, 0, k - 2)
            l0_product(0, 0, L0_TILES - 1)
            for a in range(2):
                select_fields(0, 0, a)
            pe.wait_ge(w1_low_ready, 1)
            pe.wait_ge(w2_in, DMA_INC)

            def free_of_step_before(blk, q, back):
                n = PER_BLOCK * blk + q
                if is_step(blk, q, 0) or is_step(blk, q, 1):
                    pe.wait_ge(z0_ready, L0_TILES * (n + 1) + 1 - back)
                else:
                    pe.wait_ge(g_ready, SUB * (n - 1) + 1 - back)

            def steps(blk):
                for q in range(PER_BLOCK):
                    n = PER_BLOCK * blk + q
                    t = n + 1
                    todo = preps(blk, q)
                    for i in range(PAIRS):
                        if has_next(blk, q):
                            if i == 0:
                                if q == PER_BLOCK - 1:
                                    pe.wait_ge(parts_ready, t + 4)
                                free_of_step_before(blk, q, 2)
                                l0_select(t, 0)
                                free_of_step_before(blk, q, 1)
                                l0_select(t, 1)
                            for k in range(L0_TILES):
                                if i == 2 + k // 2:
                                    l0_product(t, (q + 1) % 2, k)
                            for k in range(2, L0_TILES + 1):
                                if i == k // 2:
                                    if k == 2:
                                        pe.wait_ge(x0_rep_ready, t + 1)
                                    else:
                                        pe.wait_ge(z0_ready, L0_TILES * t + k - 2)
                                    l0_select(t, k)
                        for c, (quarter, number) in enumerate(todo):
                            if i == (5, 8)[c]:
                                pe.wait_ge(z0_ready, L0_TILES * t + 6 + c)
                                turn_quarter(number, bank_s[c])
                        if not is_step(blk, q, 0):
                            if i == 10:
                                if todo:
                                    pe.wait_ge(rest_ready, todo[0][1] + 1)
                                elif has_next(blk, q):
                                    pe.wait_ge(z0_ready, L0_TILES * t + 6)
                                else:
                                    free_of_step_before(blk, q, 2)
                                turn_x0(n)
                            if i == 11:
                                if todo:
                                    pe.wait_ge(rest_ready, todo[1][1] + 1)
                                elif has_next(blk, q):
                                    pe.wait_ge(z0_ready, L0_TILES * t + 7)
                                else:
                                    free_of_step_before(blk, q, 1)
                                turn_x2(n, (q - 1) % 2)
                            if 13 <= i < 13 + SUB:
                                g_product(n, i - 13)
                            if q % 2 and not is_step(blk, q, 1):
                                for j in range(3 * i, min(3 * i + 3, FIELDS)):
                                    l2_product(2 * blk + (q - 3) // 2, j)
                        if i % A_PAIRS == 2:
                            a = i // A_PAIRS
                            if a + 2 < A_GROUPS or has_next(blk, q):
                                pe.wait_ge(z_ready, PAIRS * n + A_PAIRS * (a + 1))
                                if a + 2 < A_GROUPS:
                                    select_fields(n, q % 2, a + 2)
                                else:
                                    select_fields(t, (q + 1) % 2, a + 2 - A_GROUPS)
                        if i == 0:
                            wait(pe, x2_ready, n - 1)
                        high_products(n, q, i)
                        late = before(blk, q, i, 1)
                        if late is not None:
                            low_products(late)

            steps(0)
            with pe.Fori(1, BLOCKS - 1) as blk:
                steps(blk)
            steps(BLOCKS - 1)
            low_products((BLOCKS - 1, PER_BLOCK - 1, PAIRS - 1))

            def top1(m, c, start=False, stop=False):
                rows = P if c < 3 else DIM
                rhs = res[:, c, :] if c < 3 else dense_sb[:]
                return mm(bank_h1[m][:], wt1_sb[0:rows, c, m * P:(m + 1) * P], rhs, start=start, stop=stop)

            pe.wait_ge(top_in, 3 * DMA_INC)
            pe.wait_ge(dense_in, DMA_INC)
            pe.wait_ge(x1_pooled, STEPS)
            for m in range(TOP1 // P):
                top1(m, 0, start=True)
                top1(m, 3)
            free_of_step_before(BLOCKS, 0, 2)
            turn_x0(STEPS)
            free_of_step_before(BLOCKS, 0, 1)
            turn_x2(STEPS, (STEPS - 1) % 2)
            pe.wait_ge(x2_pooled, STEPS)
            for m in range(TOP1 // P):
                top1(m, 1)
            for sub in range(SUB):
                g_product(STEPS, sub)
            for j in range(FIELDS):
                l2_product(STEPS // 2 - 1, j)
            pe.wait_ge(res2_ready, STEPS // 2)
            for m in range(TOP1 // P):
                top1(m, 2, stop=True).then_inc(h1_done, 1)
            for m in range(TOP2 // P):
                for c in range(TOP1 // P):
                    if m == 0:
                        pe.wait_ge(h1_ready, c + 1)
                    last = mm(bank_s[m][:], wt2_sb[:, c, m * P:(m + 1) * P], h1[:, c, :], start=(c == 0), stop=(c == 3))
                last.then_inc(h2_done, 1)
            for c in range(TOP2 // P):
                pe.wait_ge(h2_ready, c + 1)
                last = mm(bank_r2[0:1, :], wt3_sb[:, c:c + 1], h2[:, c, :], start=(c == 0), stop=(c == 1))
            last.then_inc(y_done, 1)


def layouts(v):
    f = np.arange(FIELDS)
    w0 = v["L0_rec_W0"].reshape(HID, FIELDS, FIELDS)
    w0a = np.zeros((STACK, L0_TILES, HID), np.float32)
    w0b = np.zeros((STACK, L0_TILES, HID), np.float32)
    sel0 = np.zeros((STACK, L0_TILES + 1, STACK), np.float32)
    for part in range(PARTS):
        for rep in range(PARTS):
            sel0[part * FIELDS + f, 0, rep * FIELDS + f] = 1
    shifts = list(range(1, FIELDS // 2 + 1)) + [0]
    for n, shift in enumerate(shifts):
        tile, rep = divmod(n, PARTS)
        g = (f + shift) % FIELDS
        w0a[rep * FIELDS + f, tile] = w0[:, f, g].T
        if shift:
            w0b[rep * FIELDS + f, tile] = w0[:, g, f].T
        for part in range(PARTS):
            sel0[part * FIELDS + g, tile + 1, rep * FIELDS + f] = 1
    selA = np.zeros((STACK, A_GROUPS, P), np.float32)
    for a in range(A_GROUPS):
        for p in range(P):
            j = J_GROUP * a + p % J_GROUP
            if j < FIELDS:
                selA[[j, j + FIELDS, j + 2 * FIELDS], a, p] = 1
    selT = np.tile(np.eye(FIELDS, dtype=np.float32), (PARTS, 1))
    w1 = np.zeros((HID, A_GROUPS * J_GROUP, HID), np.float32)
    w1[:, :FIELDS] = v["L0_rec_W1"].reshape(HID, FIELDS, HID)
    w1 = w1.reshape(HID, A_GROUPS, J_GROUP, B_GROUPS, K_GROUP).transpose(4, 2, 1, 3, 0).reshape(P, -1)
    return {
        "ids": v["ids"].reshape(BLOCKS, P, FIELDS).transpose(1, 0, 2),
        "dense": v["dense_ctx"].T,
        "w0a": w0a,
        "w0b": w0b.reshape(STACK, -1),
        "w1": w1,
        "w2": v["L0_rec_W2"].reshape(HID, FIELDS, HID).transpose(2, 1, 0),
        "wt1": v["W_top1"],
        "wt2": v["W_top2"],
        "wt3": v["W_top3"].reshape(TOP2 // P, P).T,
        "bias": np.stack([v["L0_rec_b0"], v["L0_rec_b1"], v["L0_rec_b2"]], axis=1),
        "bt1": v["b_top1"].reshape(TOP1 // P, P).T,
        "bt2": v["b_top2"].reshape(TOP2 // P, P).T,
        "selections": np.concatenate([sel0.reshape(STACK, -1), selA.reshape(STACK, -1), selT], axis=1),
        "mask": np.repeat(np.eye(SUB_ROWS, dtype=np.float32), DIM, axis=0),
        "eye": np.eye(P, dtype=np.float32),
    }


def kernel(**inputs):
    import concourse.bacc as bacc
    from concourse.bass_utils import run_bass_kernel_spmd

    v = {k: np.asarray(a) for k, a in inputs.items()}
    nc = bacc.Bacc("TRN2", target_bir_lowering=False, num_devices=1)
    arrays = {}

    def given(name, a):
        arrays[name] = np.ascontiguousarray(a)
        return nc.dram_tensor(name, a.shape, mybir.dt.from_np(a.dtype), kind="ExternalInput").ap()

    args = {k: given(f"in_{k}", a) for k, a in layouts(v).items()}
    tables = [given(f"in_tbl_{f}", v[f"tbl_{f}"]) for f in range(FIELDS)]
    out = nc.dram_tensor("out_y", (BATCH, 1), F32, kind="ExternalOutput").ap()
    build(nc, tables=tables, out=out, **args)
    return run_bass_kernel_spmd(nc, [arrays], core_ids=[0]).results[0]["out_y"]
```

```python
from contextlib import ExitStack

import numpy as np

import concourse.bass as bass
from concourse import mybir

F32 = mybir.dt.float32
F32R = mybir.dt.float32r
BF16 = mybir.dt.bfloat16
I32 = mybir.dt.int32
ALU = mybir.AluOpType
ACT = mybir.ActivationFunctionType
AX = mybir.AxisListType

BATCH, FIELDS, DIM, HID = 512, 39, 16, 128
P = 128
TILE = 512
ROWS = TILE // DIM
STEPS = BATCH // ROWS
BLOCKS = BATCH // P
PER_BLOCK = STEPS // BLOCKS
PARTS = 3
STACK = PARTS * FIELDS
L0_TILES = 7
J_GROUP, K_GROUP = 8, 16
A_GROUPS = -(-FIELDS // J_GROUP)
B_GROUPS = HID // K_GROUP
PAIRS = A_GROUPS * B_GROUPS // 2
A_PAIRS = B_GROUPS // 2
RING, RING_LOW = 5, 4
SUB = TILE // P
SUB_ROWS = P // DIM
QUART = DIM // 4
TOP1, TOP2 = 512, 256
L2_ROWS = 2 * ROWS
DMA_INC = 16
CONSTANTS = 7
SEL0, SELA = (L0_TILES + 1) * STACK, A_GROUPS * P
SEL_COLUMNS = SEL0 + SELA + FIELDS


def pool_doubles(block):
    return 14 if block == BLOCKS - 1 else 12


def takers(first_step, last_block):
    n = 0 if first_step else pool_doubles(BLOCKS - 1 if last_block else 0)
    return ["pool" if (i + 1) * n // PAIRS > i * n // PAIRS else "dve" for i in range(PAIRS)]


def build(nc, ids, tables, dense, w0a, w0b, w1, w2, wt1, wt2, wt3, bias, bt1, bt2, selections, mask, eye, out):
    ctx = ExitStack()
    with ctx:
        def sb(name, shape, dt=F32):
            return ctx.enter_context(nc.sbuf_tensor(name, shape, dt))

        def sem(name):
            return ctx.enter_context(nc.semaphore(name))

        idx = sb("idx", [P, BLOCKS, FIELDS], I32)
        emb = sb("emb", [P, 2, FIELDS * DIM])
        parts = sb("parts", [STACK, BATCH * DIM], BF16)
        w1_high = sb("w1_high", [P, A_GROUPS * B_GROUPS, HID], F32R)
        w1_low = sb("w1_low", [P, A_GROUPS * B_GROUPS, HID], F32R)
        w0_sb = sb("w0_sb", [STACK, L0_TILES, HID])
        w2_sb = sb("w2_sb", [P, FIELDS, HID])
        Z = sb("Z", [P, RING, 2 * TILE])
        Z_high = sb("Z_high", [P, RING, 2 * TILE], F32R)
        Z_low = sb("Z_low", [P, RING_LOW, 2 * TILE], F32R)
        z0 = sb("z0", [STACK, 2, TILE])
        x0_rep = sb("x0_rep", [STACK, TILE])
        x1 = sb("x1", [P, TILE])
        x1_rep = sb("x1_rep", [P, B_GROUPS, TILE])
        x2 = sb("x2", [P, 2, TILE])
        x2T = sb("x2T", [P, SUB, P])
        x0_diag = sb("x0_diag", [P, SUB, SUB_ROWS, FIELDS])
        G = sb("G", [P, FIELDS, L2_ROWS])
        res = sb("res", [P, 3, BATCH])
        dense_sb = sb("dense_sb", [DIM, BATCH])
        stage = sb("stage", [P, QUART, PARTS, FIELDS])
        part_high = sb("part_high", [STACK, P, QUART], BF16)
        part_mid = sb("part_mid", [STACK, P, QUART], BF16)
        rest = sb("rest", [STACK, P, QUART])
        sel_sb = sb("sel_sb", [STACK, SEL_COLUMNS], BF16)
        sel0_sb = sel_sb[:, 0:SEL0].rearrange("p (t m) -> p t m", m=STACK)
        selA_sb = sel_sb[:, SEL0:SEL0 + SELA].rearrange("p (a m) -> p a m", m=P)
        selT_sb = sel_sb[:, SEL0 + SELA:SEL_COLUMNS]
        mask_sb = sb("mask_sb", [P, SUB_ROWS])
        eye_sb = sb("eye_sb", [P, P])
        bias_sb = sb("bias_sb", [P, 4])
        bt1_sb = sb("bt1_sb", [P, TOP1 // P])
        bt2_sb = sb("bt2_sb", [P, TOP2 // P])
        wt3_sb = sb("wt3_sb", [P, TOP2 // P])
        y_sb = sb("y_sb", [1, BATCH])
        w1_stage = Z[:].rearrange("p r c -> p (r c)")[:, 0:A_GROUPS * B_GROUPS * HID]
        sel_stage = G[:].rearrange("p j b -> p (j b)")[0:STACK, 0:SEL_COLUMNS]
        w0b_stage = x0_diag[:].rearrange("p s b j -> p (s b j)")[0:STACK, 0:L0_TILES * HID]
        first = x1_rep[:].rearrange("p b c -> p (b c)").rearrange("p (m c) -> p m c", m=4)
        HALF = P * QUART // 2

        def as_quarter(ap):
            return ap.rearrange("p (b d) -> p b d", d=QUART)

        first_stage = [ap[:, 0:QUART * PARTS * FIELDS].rearrange("p (d a f) -> p d a f", d=QUART, a=PARTS) for ap in
                       (x1[:], x2[:, 0, :], x2[:, 1, :], x2T[:].rearrange("p a b -> p (a b)"))]
        first_rest = [as_quarter(first[0:STACK, m, 0:P * QUART]) for m in range(4)]
        first_high = [as_quarter(first[0:STACK, m, 2 * HALF:3 * HALF].bitcast(BF16)) for m in range(4)]
        first_mid = [as_quarter(first[0:STACK, m, 3 * HALF:4 * HALF].bitcast(BF16)) for m in range(4)]
        top_flat = x1_rep[:].rearrange("p b c -> p (b c)")
        wt1_sb = top_flat[:, 0:4 * TOP1].rearrange("p (c n) -> p c n", c=4)
        wt2_sb = top_flat[:, 4 * TOP1:4 * TOP1 + TOP1 // P * TOP2].rearrange("p (c n) -> p c n", c=TOP1 // P)
        h_flat = Z[:].rearrange("p r c -> p (r c)")
        h1 = h_flat[:, 0:TOP1 // P * BATCH].rearrange("p (c n) -> p c n", c=TOP1 // P)
        h2 = h_flat[:, TOP1 // P * BATCH:(TOP1 + TOP2) // P * BATCH].rearrange("p (c n) -> p c n", c=TOP2 // P)

        bank = [ctx.enter_context(nc.psum_tensor(f"bank{i}", [P, TILE], F32)) for i in range(8)]
        bank_a, bank_s, bank_x1, bank_x2, bank_r2 = bank[0:2], bank[2:4], bank[4], [bank[5], bank[7]], bank[6]
        bank_h1 = [bank[0], bank[1], bank[4], bank[5]]

        idx_in, w1_in, w0_in, w0b_in, w2_in = (sem(n) for n in ("idx_in", "w1_in", "w0_in", "w0b_in", "w2_in"))
        const_in, dense_in, top_in, y_out = (sem(n) for n in ("const_in", "dense_in", "top_in", "y_out"))
        gathered = [sem("gathered0"), sem("gathered1")] + [sem("gathered_later")] * (BLOCKS - 2)
        w1_high_ready, w1_low_ready, w0_ready, bias_ready, sel_ready = (
            sem(n) for n in ("w1_high_ready", "w1_low_ready", "w0_ready", "bias_ready", "sel_ready"))
        stage_ready = sem("stage_ready")
        first_staged = sem("first_staged")
        turned = sem("turned")
        high_ready = sem("high_ready")
        rest_ready = sem("rest_ready")
        mid_ready = sem("mid_ready")
        low_ready = sem("low_ready")
        mid_stacked = sem("mid_stacked")
        parts_ready = sem("parts_ready")
        l0_spread = sem("l0_spread")
        x0_rep_ready = sem("x0_rep_ready")
        z0_ready = sem("z0_ready")
        l0_done = sem("l0_done")
        x1_ready = sem("x1_ready")
        x1_spread = [sem(f"x1_spread{i}") for i in range(A_PAIRS)]
        x1_pooled = sem("x1_pooled")
        a_ready = sem("a_ready")
        z_ready = sem("z_ready")
        z_high_ready = sem("z_high_ready")
        z_low_dve = sem("z_low_dve")
        z_low_pool = sem("z_low_pool")
        used = sem("used")
        x2_ready = sem("x2_ready")
        x2_pooled = sem("x2_pooled")
        x0_turned = sem("x0_turned")
        x2_turned = sem("x2_turned")
        diag_ready = sem("diag_ready")
        x2T_ready = sem("x2T_ready")
        g_done = sem("g_done")
        g_ready = sem("g_ready")
        l2_done = sem("l2_done")
        res2_ready = sem("res2_ready")
        h1_done, h1_ready, h2_done, h2_ready, y_done, y_ready = (
            sem(n) for n in ("h1_done", "h1_ready", "h2_done", "h2_ready", "y_done", "y_ready"))

        def wait(eng, semaphore, value):
            if not isinstance(value, int) or value > 0:
                eng.wait_ge(semaphore, value)

        def part_wait(eng):
            eng.wait_ge(const_in, CONSTANTS * DMA_INC)

        def taker(blk, q, i):
            return takers(isinstance(blk, int) and blk == 0 and q == 0, isinstance(blk, int) and blk == BLOCKS - 1)[i]

        def low_count(who, blk, q, i):
            if not isinstance(blk, int):
                per_block = low_count(who, 2, 0, -1) - low_count(who, 1, 0, -1)
                return (blk - 1) * per_block + low_count_in(who, 1, q, i)
            return low_count_in(who, blk, q, i)

        def low_count_in(who, blk, q, i):
            n = 0
            for step in range(PER_BLOCK * blk + q + 1):
                kinds = takers(step == 0, step // PER_BLOCK == BLOCKS - 1)
                n += sum(k == who for k in (kinds if step < PER_BLOCK * blk + q else kinds[:i + 1]))
            return n

        def before(blk, q, i, back):
            i -= back
            if i < 0:
                i, q = i + PAIRS, q - 1
            if q < 0:
                if isinstance(blk, int) and blk == 0:
                    return None
                q += PER_BLOCK
                blk = blk - 1
            return blk, q, i

        def wait_low(eng, blk, q, i):
            if isinstance(blk, int):
                who = takers(blk == 0 and q == 0, blk == BLOCKS - 1)[i]
            else:
                who = takers(False, False)[i]
            eng.wait_ge(z_low_pool if who == "pool" else z_low_dve, low_count(who, blk, q, i))

        def preps(blk, q):
            if q not in (1, 2) or (isinstance(blk, int) and blk == BLOCKS - 1):
                return []
            return [(2 * (q - 1) + c, 4 * (blk + 1) + 2 * (q - 1) + c) for c in range(2)]

        def has_next(blk, q):
            return not (isinstance(blk, int) and PER_BLOCK * blk + q == STEPS - 1)

        def is_step(blk, q, n):
            return isinstance(blk, int) and PER_BLOCK * blk + q == n

        def block_columns(blk):
            return parts[:, bass.ds(blk * (P * DIM), P * DIM)].rearrange("p (b d) -> p b d", d=DIM)

        block = ctx.enter_context(nc.Block())

        @block.sync
        def _(sp):
            sp.dma_start(idx[:], ids).then_inc(idx_in, DMA_INC)
            for dst, src in ((eye_sb[:], eye), (sel_stage, selections), (mask_sb[:], mask),
                             (bias_sb[:, 0:3], bias), (bt1_sb[:], bt1), (bt2_sb[:], bt2), (wt3_sb[:], wt3)):
                sp.dma_start(dst, src).then_inc(const_in, DMA_INC)
            sp.dma_start(w1_stage, w1).then_inc(w1_in, DMA_INC)
            sp.dma_start(w0_sb[:], w0a).then_inc(w0_in, DMA_INC)
            sp.dma_start(w0b_stage, w0b).then_inc(w0b_in, DMA_INC)
            sp.dma_start(dense_sb[:], dense).then_inc(dense_in, DMA_INC)
            sp.dma_start(w2_sb[:], w2).then_inc(w2_in, DMA_INC)
            def spread_x1(t):
                if isinstance(t, int) and t == 0:
                    sp.wait_ge(x1_ready, 1)
                for pair in range(A_PAIRS):
                    wait(sp, z_ready, PAIRS * (t - 1) + PAIRS - A_PAIRS + pair + 1 if has_tile_before(t) else 0)
                    for b in (2 * pair, 2 * pair + 1):
                        rows = x1[K_GROUP * b:K_GROUP * (b + 1), :]
                        sp.dma_start(x1_rep[:, b, :], rows.unsqueeze(1).to_broadcast([K_GROUP, J_GROUP, TILE])
                                     ).then_inc(x1_spread[pair], DMA_INC)

            def has_tile_before(t):
                return not (isinstance(t, int) and t == 0)

            def steps(blk):
                for q in range(PER_BLOCK):
                    if has_next(blk, q):
                        spread_x1(PER_BLOCK * blk + q + 1)

            spread_x1(0)
            steps(0)
            with sp.Fori(1, BLOCKS - 1) as blk:
                steps(blk)
            steps(BLOCKS - 1)
            sp.wait_ge(z_ready, PAIRS * STEPS)
            sp.dma_start(wt1_sb[:, 0:3, :], wt1[0:3 * P, :].rearrange("(c p) n -> p c n", p=P)).then_inc(top_in, DMA_INC)
            sp.dma_start(wt1_sb[0:DIM, 3, :], wt1[3 * P:3 * P + DIM, :]).then_inc(top_in, DMA_INC)
            sp.dma_start(wt2_sb, wt2.rearrange("(c p) n -> p c n", p=P)).then_inc(top_in, DMA_INC)
            sp.wait_ge(y_ready, 1)
            sp.dma_start(out.rearrange("b o -> o b"), y_sb[:]).then_inc(y_out, DMA_INC)
            sp.wait_ge(y_out, DMA_INC)

        @block.gpsimd
        def _(pool):
            def gather(blk, f):
                pool.indirect_dma_start(emb[:, blk % 2, f * DIM:(f + 1) * DIM], None, tables[f],
                                        bass.IndirectOffsetOnAxis(ap=idx[:, blk, f:f + 1], axis=0)
                                        ).then_inc(gathered[blk], DMA_INC)

            pool.wait_ge(idx_in, DMA_INC)
            todo = [(b, f) for b in range(2, BLOCKS) for f in range(FIELDS)]
            for b in range(2):
                for f in range(FIELDS):
                    gather(b, f)
            for step in range(STEPS):
                blk, q = divmod(step, PER_BLOCK)
                for i in range(PAIRS):
                    if taker(blk, q, i) == "pool":
                        pool.wait_ge(z_high_ready, PAIRS * step + i + 1)
                        wait(pool, used, PAIRS * step + i + 1 - RING_LOW)
                        pool.tensor_tensor(Z_low[:, i % RING_LOW, :], Z[:, i % RING, :],
                                           Z_high[:, i % RING, :].bitcast(F32), ALU.subtract).then_inc(z_low_pool, 1)
                    if step and i % 2 == 0 and todo:
                        b, f = todo.pop(0)
                        if f == 0:
                            pool.wait_ge(turned, 4 * (b - 1))
                            wait(pool, gathered[b], (b - 2) * FIELDS * DMA_INC)
                        gather(b, f)

        @block.scalar
        def _(act):
            def copy(dst, src):
                return nc.scalar.copy(dst, src)

            def stage_quarter(rows, quarter, number):
                part_wait(act)
                wait(act, turned, number)
                src = rows.rearrange("p (f d) -> p d f", d=DIM)[:, QUART * quarter:QUART * (quarter + 1), :]
                copy(stage[:], src.unsqueeze(2).to_broadcast([P, QUART, PARTS, FIELDS])).then_inc(stage_ready, 1)

            def quarter_high(number, src, dst):
                act.wait_ge(turned, number + 1)
                if dst is part_high:
                    wait(act, parts_ready, number)
                copy(dst[:], src[0:STACK, :].rearrange("p (d b) -> p b d", d=QUART)).then_inc(high_ready, 1)

            def quarter_mid(number, src, dst):
                act.wait_ge(rest_ready, number + 1)
                copy(dst[:], src[:]).then_inc(mid_ready, 1)

            def quarter_stack(blk, quarter, number):
                cols = block_columns(blk)[:, :, QUART * quarter:QUART * (quarter + 1)]
                part_wait(act)
                act.wait_ge(low_ready, number + 1)
                copy(cols[0:2 * FIELDS], part_mid[0:2 * FIELDS]).then_inc(mid_stacked, 1)
                part_wait(act)
                act.wait_ge(mid_stacked, number + 1)
                copy(cols[0:FIELDS], part_high[0:FIELDS]).then_inc(parts_ready, 1)

            def evacuate_x0_rep(t):
                act.wait_ge(l0_spread, (L0_TILES + 1) * t + 1)
                wait(act, z0_ready, L0_TILES * t)
                copy(x0_rep[:], bank_s[0][0:STACK, :]).then_inc(x0_rep_ready, 1)

            def evacuate_x1(t):
                act.wait_ge(l0_done, L0_TILES * (t + 1))
                wait(act, x1_pooled, t)
                nc.scalar.activation(x1[:], bank_x1[:], ACT.Identity, bias=bias_sb[:, 0:1]).then_inc(x1_ready, 1)

            def diagonal(n):
                act.wait_ge(x0_turned, n)
                wait(act, g_done, SUB * (n - 1))
                x0_cols = bank_s[0][:, 0:SUB * FIELDS].rearrange("p (s j) -> p s j", j=FIELDS)
                for b in range(SUB_ROWS):
                    last = nc.scalar.activation(x0_diag[:, :, b, :], x0_cols, ACT.Copy, scale=mask_sb[:, b:b + 1])
                last.then_inc(diag_ready, 1)

            def evacuate_x2(n, parity):
                act.wait_ge(used, PAIRS * n)
                wait(act, x2_turned, n - 2)
                wait(act, x2_pooled, n - 2)
                nc.scalar.activation(x2[:, parity, :], bank_x2[parity][:], ACT.Identity,
                                     bias=bias_sb[:, 1:2]).then_inc(x2_ready, 1)

            def evacuate_x2T(n):
                act.wait_ge(x2_turned, n)
                wait(act, g_done, SUB * (n - 1))
                copy(x2T[:].rearrange("p a b -> p (a b)"), bank_s[1][:]).then_inc(x2T_ready, 1)

            def evacuate_g(n, parity, sub, l2_before):
                act.wait_ge(g_done, SUB * (n - 1) + sub + 1)
                if parity == 0 and sub == 0:
                    wait(act, l2_done, l2_before)
                at = ROWS * parity + SUB_ROWS * sub
                copy(G[:, :, at:at + SUB_ROWS].rearrange("p j b -> p b j"),
                     bank_s[sub % 2][:, 0:SUB_ROWS * FIELDS].rearrange("p (b j) -> p b j", j=FIELDS)
                     ).then_inc(g_ready, 1)

            def evacuate_res2(number):
                part_wait(act)
                act.wait_ge(l2_done, number + 1)
                nc.scalar.activation(res[:, 2, bass.ds(number * L2_ROWS, L2_ROWS)], bank_r2[:, 0:L2_ROWS], ACT.Identity,
                                     bias=bias_sb[:, 3:4]).then_inc(res2_ready, 1)

            act.wait_ge(const_in, CONSTANTS * DMA_INC)
            nc.scalar.mul(bias_sb[:, 3:4], bias_sb[:, 2:3], float(DIM)).then_inc(bias_ready, 1)
            copy(sel_sb[:], sel_stage).then_inc(sel_ready, 1)
            act.wait_ge(w1_in, DMA_INC)
            copy(w1_high[:].rearrange("p t h -> p (t h)"), w1_stage).then_inc(w1_high_ready, 1)
            for m in range(4):
                quarter_high(m, bank[m], first_high[m])
            for m in range(4):
                quarter_mid(m, first_rest[m], first_mid[m])
            for m in range(4):
                act.wait_ge(mid_stacked, m + 1)
                copy(block_columns(0)[0:FIELDS, :, QUART * m:QUART * (m + 1)], first_high[m][0:FIELDS]).then_inc(parts_ready, 1)
            evacuate_x0_rep(0)
            evacuate_x1(0)
            act.wait_ge(bias_ready, 1)

            def steps(blk, next_rows=None, next_gathered=None, next_count=None):
                for q in range(PER_BLOCK):
                    n = PER_BLOCK * blk + q
                    t = n + 1
                    todo = preps(blk, q)
                    for i in range(PAIRS):
                        if i == 4 and not is_step(blk, q, 0):
                            evacuate_x2(n, (q - 1) % 2)
                        if i == 3 and has_next(blk, q):
                            evacuate_x0_rep(t)
                        if i == 12 and has_next(blk, q):
                            evacuate_x1(t)
                        for c, (quarter, number) in enumerate(todo):
                            if i == (3, 11)[c]:
                                if quarter == 0:
                                    act.wait_ge(next_gathered, next_count)
                                stage_quarter(next_rows, quarter, number)
                            if i == (11, 15)[c]:
                                quarter_high(number, bank_s[c], part_high)
                            if i == (12, 16)[c]:
                                quarter_mid(number, rest, part_mid)
                            if i == (14, 18)[c]:
                                quarter_stack(blk + 1, quarter, number)
                        if not is_step(blk, q, 0):
                            if i == 15:
                                diagonal(n)
                                evacuate_x2T(n)
                            if q % 2 and i == 16 and not is_step(blk, q, 1):
                                evacuate_res2(2 * blk + (q - 3) // 2)
                            if i >= 16:
                                evacuate_g(n, (q - 1) % 2, i - 16, 2 * blk + (q - 1) // 2)
                        act.wait_ge(z_ready, PAIRS * n + i + 1)
                        wait(act, used, PAIRS * n + i + 1 - RING)
                        copy(Z_high[:, i % RING, :], Z[:, i % RING, :]).then_inc(z_high_ready, 1)

            steps(0, emb[:, 1, :], gathered[1], FIELDS * DMA_INC)
            emb_flat = emb[:].rearrange("p a b -> p (a b)")
            with act.Fori(1, BLOCKS - 1) as blk:
                steps(blk, emb_flat[:, bass.ds((blk - 1) * (FIELDS * DIM), FIELDS * DIM)],
                      gathered[2], blk * (FIELDS * DMA_INC))
            steps(BLOCKS - 1)

            n = STEPS
            evacuate_x2(n, (n - 1) % 2)
            diagonal(n)
            evacuate_x2T(n)
            for sub in range(SUB):
                evacuate_g(n, (n - 1) % 2, sub, 0)
            evacuate_res2(STEPS // 2 - 1)
            for m in range(TOP1 // P):
                act.wait_ge(h1_done, m + 1)
                nc.scalar.activation(h1[:, m, :], bank_h1[m][:], ACT.Relu, bias=bt1_sb[:, m:m + 1]).then_inc(h1_ready, 1)
            for m in range(TOP2 // P):
                act.wait_ge(h2_done, m + 1)
                nc.scalar.activation(h2[:, m, :], bank_s[m][:], ACT.Relu, bias=bt2_sb[:, m:m + 1]).then_inc(h2_ready, 1)
            act.wait_ge(y_done, 1)
            copy(y_sb[:], bank_r2[0:1, :]).then_inc(y_ready, 1)

        @block.vector
        def _(dve):
            def quarter_rest(number, src, high, dst):
                dve.wait_ge(high_ready, number + 1)
                if dst is rest:
                    wait(dve, low_ready, number)
                nc.vector.tensor_tensor(dst[:], src[0:STACK, :].rearrange("p (d b) -> p b d", d=QUART), high[:],
                                        ALU.subtract).then_inc(rest_ready, 1)

            def quarter_low(blk, quarter, number, src, mid):
                cols = block_columns(blk)[:, :, QUART * quarter:QUART * (quarter + 1)]
                dve.wait_ge(mid_ready, number + 1)
                nc.vector.tensor_tensor(cols, src[:], mid[:], ALU.subtract).then_inc(low_ready, 1)

            def l0_pairs(t, t_parity, k):
                if k == 0:
                    dve.wait_ge(x0_rep_ready, t + 1)
                dve.wait_ge(l0_spread, (L0_TILES + 1) * t + k + 2)
                wait(dve, l0_done, L0_TILES * t + k - 1)
                nc.vector.tensor_tensor(z0[:, (t_parity + k) % 2, :], bank_s[(k + 1) % 2][0:STACK, :], x0_rep[:],
                                        ALU.mult).then_inc(z0_ready, 1)

            def pool_x1(t):
                part_wait(dve)
                dve.wait_ge(x1_ready, t + 1)
                nc.vector.reduce_sum(res[:, 0, bass.ds(t * ROWS, ROWS)],
                                     x1[:].rearrange("p (b d) -> p b d", d=DIM), AX.X).then_inc(x1_pooled, 1)

            def pool_x2(n, parity):
                part_wait(dve)
                dve.wait_ge(x2_ready, n)
                nc.vector.reduce_sum(res[:, 1, bass.ds((n - 1) * ROWS, ROWS)],
                                     x2[:, parity, :].rearrange("p (b d) -> p b d", d=DIM), AX.X).then_inc(x2_pooled, 1)

            def low_part(at):
                blk, q, i = at
                n = PER_BLOCK * blk + q
                dve.wait_ge(z_high_ready, PAIRS * n + i + 1)
                wait(dve, used, PAIRS * n + i + 1 - RING_LOW)
                nc.vector.tensor_tensor(Z_low[:, i % RING_LOW, :], Z[:, i % RING, :], Z_high[:, i % RING, :].bitcast(F32),
                                        ALU.subtract).then_inc(z_low_dve, 1)

            dve.wait_ge(w0_in, DMA_INC)
            dve.wait_ge(w0b_in, DMA_INC)
            w0_flat = w0_sb[:].rearrange("p t h -> p (t h)")
            nc.vector.tensor_tensor(w0_flat, w0_flat, w0b_stage, ALU.add).then_inc(w0_ready, 1)
            dve.wait_ge(w1_high_ready, 1)
            nc.vector.tensor_tensor(w1_low[:].rearrange("p t h -> p (t h)"), w1_stage,
                                    w1_high[:].rearrange("p t h -> p (t h)").bitcast(F32), ALU.subtract).then_inc(w1_low_ready, 1)
            dve.wait_ge(gathered[0], FIELDS * DMA_INC)
            first_rows = emb[:, 0, :].rearrange("p (f d) -> p d f", d=DIM)
            for m in range(4):
                nc.vector.tensor_copy(first_stage[m], first_rows[:, QUART * m:QUART * (m + 1), :].unsqueeze(2)
                                      .to_broadcast([P, QUART, PARTS, FIELDS])).then_inc(first_staged, 1)
            for m in range(4):
                quarter_rest(m, bank[m], first_high[m], first_rest[m])
            for m in range(4):
                quarter_low(0, m, m, first_rest[m], first_mid[m])
                dve.wait_ge(low_ready, m + 1)
                nc.vector.tensor_copy(block_columns(0)[0:2 * FIELDS, :, QUART * m:QUART * (m + 1)],
                                      first_mid[m][0:2 * FIELDS]).then_inc(mid_stacked, 1)
            dve.wait_ge(const_in, CONSTANTS * DMA_INC)
            for k in range(L0_TILES):
                l0_pairs(0, 0, k)
            pool_x1(0)

            def steps(blk):
                for q in range(PER_BLOCK):
                    n = PER_BLOCK * blk + q
                    t = n + 1
                    todo = preps(blk, q)
                    for i in range(PAIRS):
                        if has_next(blk, q):
                            for k in range(L0_TILES):
                                if i == 5 + k:
                                    l0_pairs(t, (q + 1) % 2, k)
                            if i == 14:
                                pool_x1(t)
                        if not is_step(blk, q, 0):
                            if i == 9:
                                pool_x2(n, (q - 1) % 2)
                        for c, (quarter, number) in enumerate(todo):
                            if i == (12, 16)[c]:
                                quarter_rest(number, bank_s[c], part_high, rest)
                            if i == (13, 17)[c]:
                                quarter_low(blk + 1, quarter, number, rest, part_mid)
                        a, b = i // A_PAIRS, 2 * (i % A_PAIRS)
                        if i % A_PAIRS == 0:
                            dve.wait_ge(a_ready, A_GROUPS * n + a + 1)
                        if i < A_PAIRS:
                            dve.wait_ge(x1_spread[i], 2 * DMA_INC * (n + 1))
                        last_user = before(blk, q, i, RING)
                        if last_user is not None:
                            wait_low(dve, *last_user)
                        nc.vector.tensor_tensor(
                            Z[:, i % RING, :].rearrange("p (u c) -> p u c", u=2),
                            bank_a[(q + a) % 2][:].unsqueeze(1).to_broadcast([P, 2, TILE]),
                            x1_rep[:, b:b + 2, :], ALU.mult).then_inc(z_ready, 1)
                        late = before(blk, q, i, 2)
                        if late is not None and taker_at(late) == "dve":
                            low_part(late)

            def taker_at(at):
                blk, q, i = at
                if isinstance(blk, int):
                    return takers(blk == 0 and q == 0, blk == BLOCKS - 1)[i]
                return takers(False, False)[i]

            steps(0)
            with dve.Fori(1, BLOCKS - 1) as blk:
                steps(blk)
            steps(BLOCKS - 1)
            for i in (PAIRS - 2, PAIRS - 1):
                if taker_at((BLOCKS - 1, PER_BLOCK - 1, i)) == "dve":
                    low_part((BLOCKS - 1, PER_BLOCK - 1, i))
            pool_x2(STEPS, (STEPS - 1) % 2)

        @block.tensor
        def _(pe):
            mm = nc.tensor.matmul

            def turn_quarter(src, dst):
                for d in range(QUART):
                    last = nc.tensor.transpose(dst[0:STACK, P * d:P * (d + 1)],
                                               src[:, d].rearrange("p a f -> p (a f)"), eye_sb[:])
                last.then_inc(turned, 1)

            def l0_select(t, k):
                mm(bank_s[k % 2][0:STACK, :], sel0_sb[:, k, :], parts[:, bass.ds(t * TILE, TILE)],
                   start=True, stop=True).then_inc(l0_spread, 1)

            def l0_product(t, t_parity, k):
                pe.wait_ge(z0_ready, L0_TILES * t + k + 1)
                if k == 0:
                    wait(pe, x1_ready, t)
                mm(bank_x1[:], w0_sb[:, k, :], z0[:, (t_parity + k) % 2, :],
                   start=(k == 0), stop=(k == L0_TILES - 1)).then_inc(l0_done, 1)

            def select_fields(n, n_parity, a):
                mm(bank_a[(n_parity + a) % 2][:], selA_sb[:, a, :], parts[:, bass.ds(n * TILE, TILE)],
                   start=True, stop=True).then_inc(a_ready, 1)

            def high_products(n, q, i):
                pe.wait_ge(z_high_ready, PAIRS * n + i + 1)
                for u in range(2):
                    for w in (w1_high, w1_low):
                        mm(bank_x2[q % 2][:], w[:, 2 * i + u, :], Z_high[:, i % RING, u * TILE:(u + 1) * TILE],
                           start=(i == 0 and u == 0 and w is w1_high), stop=False)

            def low_products(at):
                blk, q, i = at
                wait_low(pe, blk, q, i)
                for u in range(2):
                    last = mm(bank_x2[q % 2][:], w1_high[:, 2 * i + u, :], Z_low[:, i % RING_LOW, u * TILE:(u + 1) * TILE],
                              start=False, stop=(i == PAIRS - 1 and u == 1))
                last.then_inc(used, 1)

            def turn_x0(n):
                for s in range(SUB):
                    last = mm(bank_s[0][:, s * FIELDS:(s + 1) * FIELDS], parts[:, bass.ds((n - 1) * TILE + s * P, P)],
                              selT_sb[:], start=True, stop=True)
                last.then_inc(x0_turned, 1)

            def turn_x2(n, parity):
                pe.wait_ge(x2_ready, n)
                for s in range(SUB):
                    last = nc.tensor.transpose(bank_s[1][:, s * P:(s + 1) * P], x2[:, parity, s * P:(s + 1) * P], eye_sb[:])
                last.then_inc(x2_turned, 1)

            def g_product(n, sub):
                if sub == 0:
                    pe.wait_ge(diag_ready, n)
                    pe.wait_ge(x2T_ready, n)
                if sub >= 2:
                    pe.wait_ge(g_ready, SUB * (n - 1) + sub - 1)
                mm(bank_s[sub % 2][:, 0:SUB_ROWS * FIELDS], x2T[:, sub, :],
                   x0_diag[:, sub].rearrange("p b j -> p (b j)"), start=True, stop=True).then_inc(g_done, 1)

            def l2_product(number, j):
                if j == 0:
                    pe.wait_ge(g_ready, 2 * SUB * (number + 1))
                    wait(pe, res2_ready, number)
                last = mm(bank_r2[:, 0:L2_ROWS], w2_sb[:, j, :], G[:, j, :], start=(j == 0), stop=(j == FIELDS - 1))
                if j == FIELDS - 1:
                    last.then_inc(l2_done, 1)

            pe.wait_ge(const_in, CONSTANTS * DMA_INC)
            for m in range(4):
                pe.wait_ge(first_staged, m + 1)
                turn_quarter(first_stage[m], bank[m])
            pe.wait_ge(parts_ready, 4)
            pe.wait_ge(sel_ready, 1)
            pe.wait_ge(w0_ready, 1)
            for k in range(L0_TILES + 1):
                if k >= 3:
                    pe.wait_ge(z0_ready, k - 2)
                elif k == 2:
                    pe.wait_ge(x0_rep_ready, 1)
                l0_select(0, k)
                if k >= 2:
                    l0_product(0, 0, k - 2)
            l0_product(0, 0, L0_TILES - 1)
            for a in range(2):
                select_fields(0, 0, a)
            pe.wait_ge(w1_low_ready, 1)
            pe.wait_ge(w2_in, DMA_INC)

            def free_of_step_before(blk, q, back):
                n = PER_BLOCK * blk + q
                if is_step(blk, q, 0) or is_step(blk, q, 1):
                    pe.wait_ge(z0_ready, L0_TILES * (n + 1) + 1 - back)
                else:
                    pe.wait_ge(g_ready, SUB * (n - 1) + 1 - back)

            def steps(blk):
                for q in range(PER_BLOCK):
                    n = PER_BLOCK * blk + q
                    t = n + 1
                    todo = preps(blk, q)
                    for i in range(PAIRS):
                        if has_next(blk, q):
                            if i == 0:
                                if q == PER_BLOCK - 1:
                                    pe.wait_ge(parts_ready, t + 4)
                                free_of_step_before(blk, q, 2)
                                l0_select(t, 0)
                                free_of_step_before(blk, q, 1)
                                l0_select(t, 1)
                            for k in range(L0_TILES):
                                if i == 2 + k:
                                    l0_product(t, (q + 1) % 2, k)
                            for k in range(2, L0_TILES + 1):
                                if i == k - 1:
                                    if k == 2:
                                        pe.wait_ge(x0_rep_ready, t + 1)
                                    else:
                                        pe.wait_ge(z0_ready, L0_TILES * t + k - 2)
                                    l0_select(t, k)
                        for c, (quarter, number) in enumerate(todo):
                            if i == (7, 9)[c]:
                                pe.wait_ge(z0_ready, L0_TILES * t + 6 + c)
                                pe.wait_ge(stage_ready, number - 3)
                                turn_quarter(stage, bank_s[c])
                        if not is_step(blk, q, 0):
                            if i == 11:
                                if todo:
                                    pe.wait_ge(rest_ready, todo[0][1] + 1)
                                elif has_next(blk, q):
                                    pe.wait_ge(z0_ready, L0_TILES * t + 6)
                                else:
                                    free_of_step_before(blk, q, 2)
                                turn_x0(n)
                            if i == 12:
                                if todo:
                                    pe.wait_ge(rest_ready, todo[1][1] + 1)
                                elif has_next(blk, q):
                                    pe.wait_ge(z0_ready, L0_TILES * t + 7)
                                else:
                                    free_of_step_before(blk, q, 1)
                                turn_x2(n, (q - 1) % 2)
                            if 14 <= i < 14 + SUB:
                                g_product(n, i - 14)
                            if q % 2 and not is_step(blk, q, 1):
                                for j in range(3 * i, min(3 * i + 3, FIELDS)):
                                    l2_product(2 * blk + (q - 3) // 2, j)
                        if i % A_PAIRS == 1:
                            a = i // A_PAIRS
                            if a + 2 < A_GROUPS or has_next(blk, q):
                                pe.wait_ge(z_ready, PAIRS * n + A_PAIRS * (a + 1))
                                if a + 2 < A_GROUPS:
                                    select_fields(n, q % 2, a + 2)
                                else:
                                    select_fields(t, (q + 1) % 2, a + 2 - A_GROUPS)
                        if i == 0:
                            wait(pe, x2_ready, n - 1)
                        high_products(n, q, i)
                        late = before(blk, q, i, 1)
                        if late is not None:
                            low_products(late)

            steps(0)
            with pe.Fori(1, BLOCKS - 1) as blk:
                steps(blk)
            steps(BLOCKS - 1)
            low_products((BLOCKS - 1, PER_BLOCK - 1, PAIRS - 1))

            def top1(m, c, start=False, stop=False):
                rows = P if c < 3 else DIM
                rhs = res[:, c, :] if c < 3 else dense_sb[:]
                return mm(bank_h1[m][:], wt1_sb[0:rows, c, m * P:(m + 1) * P], rhs, start=start, stop=stop)

            pe.wait_ge(top_in, 3 * DMA_INC)
            pe.wait_ge(dense_in, DMA_INC)
            pe.wait_ge(x1_pooled, STEPS)
            for m in range(TOP1 // P):
                top1(m, 0, start=True)
                top1(m, 3)
            free_of_step_before(BLOCKS, 0, 2)
            turn_x0(STEPS)
            free_of_step_before(BLOCKS, 0, 1)
            turn_x2(STEPS, (STEPS - 1) % 2)
            pe.wait_ge(x2_pooled, STEPS)
            for m in range(TOP1 // P):
                top1(m, 1)
            for sub in range(SUB):
                g_product(STEPS, sub)
            for j in range(FIELDS):
                l2_product(STEPS // 2 - 1, j)
            pe.wait_ge(res2_ready, STEPS // 2)
            for m in range(TOP1 // P):
                top1(m, 2, stop=True).then_inc(h1_done, 1)
            for m in range(TOP2 // P):
                for c in range(TOP1 // P):
                    if m == 0:
                        pe.wait_ge(h1_ready, c + 1)
                    last = mm(bank_s[m][:], wt2_sb[:, c, m * P:(m + 1) * P], h1[:, c, :], start=(c == 0), stop=(c == 3))
                last.then_inc(h2_done, 1)
            for c in range(TOP2 // P):
                pe.wait_ge(h2_ready, c + 1)
                last = mm(bank_r2[0:1, :], wt3_sb[:, c:c + 1], h2[:, c, :], start=(c == 0), stop=(c == 1))
            last.then_inc(y_done, 1)


def layouts(v):
    f = np.arange(FIELDS)
    w0 = v["L0_rec_W0"].reshape(HID, FIELDS, FIELDS)
    w0a = np.zeros((STACK, L0_TILES, HID), np.float32)
    w0b = np.zeros((STACK, L0_TILES, HID), np.float32)
    sel0 = np.zeros((STACK, L0_TILES + 1, STACK), np.float32)
    for part in range(PARTS):
        for rep in range(PARTS):
            sel0[part * FIELDS + f, 0, rep * FIELDS + f] = 1
    shifts = list(range(1, FIELDS // 2 + 1)) + [0]
    for n, shift in enumerate(shifts):
        tile, rep = divmod(n, PARTS)
        g = (f + shift) % FIELDS
        w0a[rep * FIELDS + f, tile] = w0[:, f, g].T
        if shift:
            w0b[rep * FIELDS + f, tile] = w0[:, g, f].T
        for part in range(PARTS):
            sel0[part * FIELDS + g, tile + 1, rep * FIELDS + f] = 1
    selA = np.zeros((STACK, A_GROUPS, P), np.float32)
    for a in range(A_GROUPS):
        for p in range(P):
            j = J_GROUP * a + p % J_GROUP
            if j < FIELDS:
                selA[[j, j + FIELDS, j + 2 * FIELDS], a, p] = 1
    selT = np.tile(np.eye(FIELDS, dtype=np.float32), (PARTS, 1))
    w1 = np.zeros((HID, A_GROUPS * J_GROUP, HID), np.float32)
    w1[:, :FIELDS] = v["L0_rec_W1"].reshape(HID, FIELDS, HID)
    w1 = w1.reshape(HID, A_GROUPS, J_GROUP, B_GROUPS, K_GROUP).transpose(4, 2, 1, 3, 0).reshape(P, -1)
    return {
        "ids": v["ids"].reshape(BLOCKS, P, FIELDS).transpose(1, 0, 2),
        "dense": v["dense_ctx"].T,
        "w0a": w0a,
        "w0b": w0b.reshape(STACK, -1),
        "w1": w1,
        "w2": v["L0_rec_W2"].reshape(HID, FIELDS, HID).transpose(2, 1, 0),
        "wt1": v["W_top1"],
        "wt2": v["W_top2"],
        "wt3": v["W_top3"].reshape(TOP2 // P, P).T,
        "bias": np.stack([v["L0_rec_b0"], v["L0_rec_b1"], v["L0_rec_b2"]], axis=1),
        "bt1": v["b_top1"].reshape(TOP1 // P, P).T,
        "bt2": v["b_top2"].reshape(TOP2 // P, P).T,
        "selections": np.concatenate([sel0.reshape(STACK, -1), selA.reshape(STACK, -1), selT], axis=1),
        "mask": np.repeat(np.eye(SUB_ROWS, dtype=np.float32), DIM, axis=0),
        "eye": np.eye(P, dtype=np.float32),
    }


def kernel(**inputs):
    import concourse.bacc as bacc
    from concourse.bass_utils import run_bass_kernel_spmd

    v = {k: np.asarray(a) for k, a in inputs.items()}
    nc = bacc.Bacc("TRN2", target_bir_lowering=False, num_devices=1)
    arrays = {}

    def given(name, a):
        arrays[name] = np.ascontiguousarray(a)
        return nc.dram_tensor(name, a.shape, mybir.dt.from_np(a.dtype), kind="ExternalInput").ap()

    args = {k: given(f"in_{k}", a) for k, a in layouts(v).items()}
    tables = [given(f"in_tbl_{f}", v[f"tbl_{f}"]) for f in range(FIELDS)]
    out = nc.dram_tensor("out_y", (BATCH, 1), F32, kind="ExternalOutput").ap()
    build(nc, tables=tables, out=out, **args)
    return run_bass_kernel_spmd(nc, [arrays], core_ids=[0]).results[0]["out_y"]
```

```python
from contextlib import ExitStack

import numpy as np

import concourse.bass as bass
from concourse import mybir

F32 = mybir.dt.float32
F32R = mybir.dt.float32r
BF16 = mybir.dt.bfloat16
I32 = mybir.dt.int32
ALU = mybir.AluOpType
ACT = mybir.ActivationFunctionType
AX = mybir.AxisListType

BATCH, FIELDS, DIM, HID = 512, 39, 16, 128
P = 128
TILE = 512
ROWS = TILE // DIM
STEPS = BATCH // ROWS
BLOCKS = BATCH // P
PER_BLOCK = STEPS // BLOCKS
G_COLUMNS = FIELDS + 1
PARTS = 3
STACK = PARTS * FIELDS
L0_TILES = 7
J_GROUP, K_GROUP = 8, 16
A_GROUPS = -(-FIELDS // J_GROUP)
B_GROUPS = HID // K_GROUP
PAIRS = A_GROUPS * B_GROUPS // 2
A_PAIRS = B_GROUPS // 2
FIELDS_AT = 1
RING, RING_LOW = 5, 4
SUB = TILE // P
SUB_ROWS = P // DIM
QUART = DIM // 4
TOP1, TOP2 = 512, 256
L2_ROWS = P
LOW_LAG = 3
DMA_INC = 16
CONSTANTS = 8
SEL0, SELA = L0_TILES * P, A_GROUPS * P
SEL_COLUMNS = SEL0 + SELA + FIELDS
LAST = L0_TILES - 1
LAST_ROWS = 32
MEMBERS = L0_TILES * FIELDS
SQUARES = L0_TILES - 2
EARLY_FIELDS = 33


FIRST_BLOCK = ["DDDPDPPDPDPPDPDPPDPP",
               "DPDPPPDPPDDPPPDPPDDP",
               "PDPDPDPDPPPDPDPDPDPD",
               "PDPDPDPPPPPDPDPDPDDP"]
LOOP_BLOCKS = ["PDPDPPPDPPPDPDDPPDPD",
               "PDPDDPDPDDPDPDPDDPDD",
               "PPDPDPDPPPDPPDPDDPPD",
               "PPDPDPDPPPPPPDPDPDDP"]
LAST_BLOCK = ["PDDPPDPDPPPDPPDPPDPP",
              "DPDPDPDPDPPDPDPDPDPP",
              "DPDPPDPPDPPDPPDPPDPP",
              "DPDPPDPPDPPDPPDPPDPP"]
LOW_PARTS = FIRST_BLOCK + (BLOCKS - 2) * LOOP_BLOCKS + LAST_BLOCK
GATHERS_BEFORE = 30
GATHERS = [7, 8, 11, 9, 9, 20, 8, 8, 7] + 7 * [0]
CLOCK_BEFORE_TURNS, CLOCK_BEFORE_SUMS, CLOCK_AT_SUMS, CLOCK_BEFORE_STEPS = 18, 3, 7, 28
TURNS = {1: [(14, 0)], 2: [(2, 1), (7, 2), (12, 3)]}
TURN_LAG = 4
SPLIT_STEP, SPLIT_AT = 1, 11


def takers(step):
    return [{"D": "dve", "P": "pool"}[who] for who in LOW_PARTS[step]]


def build(nc, ids, tables, dense, w0a, w0b, w1, w2, wt1, wt1_dense, wt2, wt3, bias, bt1, bt2, selections, members,
          mask, eye, out):
    ctx = ExitStack()
    with ctx:
        def sb(name, shape, dt=F32):
            return ctx.enter_context(nc.sbuf_tensor(name, shape, dt))

        def sem(name):
            return ctx.enter_context(nc.semaphore(name))

        idx = sb("idx", [P, BLOCKS, FIELDS], I32)
        emb = sb("emb", [P, 2, FIELDS * DIM])
        parts = sb("parts", [STACK, 2 * P * DIM], BF16)
        w1_high = sb("w1_high", [P, A_GROUPS * B_GROUPS, HID], F32R)
        w1_low = sb("w1_low", [P, A_GROUPS * B_GROUPS, HID], F32R)
        w0_high = sb("w0_high", [P, L0_TILES, HID], F32R)
        w0_low = sb("w0_low", [P, L0_TILES, HID], F32R)
        w2_sb = sb("w2_sb", [P, FIELDS, HID])
        Z = sb("Z", [P, RING, 2 * TILE])
        Z_high = sb("Z_high", [P, RING, 2 * TILE], F32R)
        Z_low = sb("Z_low", [P, RING_LOW, 2 * TILE], F32R)
        z0_odd = sb("z0_odd", [P, FIELDS * DIM])
        z0_high = sb("z0_high", [P, 2, TILE], F32R)
        z0_low = sb("z0_low", [P, 2, TILE], F32R)
        x1 = sb("x1", [P, TILE])
        x1_rep = sb("x1_rep", [P, B_GROUPS, TILE])
        x2 = sb("x2", [P, TILE])
        x2T = sb("x2T", [P, SUB, P])
        x0_diag = sb("x0_diag", [P, SUB, SUB_ROWS, G_COLUMNS])
        G = sb("G", [P, G_COLUMNS, L2_ROWS])
        res = sb("res", [P, 3, BATCH])
        split_sb = sb("split_sb", [P, DIM * STACK], BF16)
        split = split_sb[:].rearrange("p (d a f) -> p d a f", d=DIM, a=PARTS)
        rest = z0_odd[:].rearrange("p (d f) -> p d f", d=DIM)
        eye_bf = sb("eye_bf", [P, P], BF16)
        sel_sb = sb("sel_sb", [STACK, SEL_COLUMNS], BF16)
        sel0_sb = sel_sb[:, 0:SEL0].rearrange("p (t m) -> p t m", m=P)
        selA_sb = sel_sb[:, SEL0:SEL0 + SELA].rearrange("p (a m) -> p a m", m=P)
        selT_sb = sel_sb[:, SEL0 + SELA:SEL_COLUMNS]
        mask_sb = sb("mask_sb", [P, SUB_ROWS])
        eye_sb = sb("eye_sb", [P, P])
        bias_sb = sb("bias_sb", [P, 4])
        bt1_sb = sb("bt1_sb", [P, TOP1 // P])
        bt2_sb = sb("bt2_sb", [P, TOP2 // P])
        wt3_sb = sb("wt3_sb", [P, TOP2 // P])
        z0 = [x2T[:].rearrange("p a b -> p (a b)"), z0_odd[:, 0:TILE]]
        w1_stage = Z[:].rearrange("p r c -> p (r c)")[:, 0:A_GROUPS * B_GROUPS * HID]
        setup_flat = G[:].rearrange("p j b -> p (j b)")
        sel_stage = setup_flat[0:STACK, 0:SEL_COLUMNS]
        members_sb = setup_flat[:, SEL_COLUMNS:SEL_COLUMNS + MEMBERS].rearrange("p (t f) -> p t f", f=FIELDS)
        sel_end = SEL_COLUMNS + MEMBERS
        w0_stage, w0b_stage = (setup_flat[:, sel_end + n * L0_TILES * HID:sel_end + (n + 1) * L0_TILES * HID]
                               for n in range(2))
        top_flat = x1_rep[:].rearrange("p b c -> p (b c)")
        wt1_sb = top_flat[:, 0:2 * TOP1].rearrange("p (c n) -> p c n", c=2)
        wt2_sb = top_flat[:, 2 * TOP1:2 * TOP1 + TOP1 // P * TOP2].rearrange("p (c n) -> p c n", c=TOP1 // P)
        emb_flat = emb[:].rearrange("p a b -> p (a b)")
        wt1_early = emb_flat[:, 0:TOP1]
        context_rows = 3 * LAST_ROWS
        context_w_stage = emb_flat[0:context_rows, TOP1:2 * TOP1]
        context_stage = split_sb[:].bitcast(F32)[0:context_rows, 0:BATCH]
        context, context_w = z0_high[0:context_rows, 0, :], z0_low[0:context_rows, 0, :]
        h_flat = Z[:].rearrange("p r c -> p (r c)")
        h1 = h_flat[:, 0:TOP1 // P * BATCH].rearrange("p (c n) -> p c n", c=TOP1 // P)
        y_sb = h_flat[0:1, (TOP1 + TOP2) // P * BATCH:((TOP1 + TOP2) // P + 1) * BATCH]
        h2 = h_flat[:, TOP1 // P * BATCH:(TOP1 + TOP2) // P * BATCH].rearrange("p (c n) -> p c n", c=TOP2 // P)

        bank = [ctx.enter_context(nc.psum_tensor(f"bank{i}", [P, TILE], F32)) for i in range(8)]
        bank_a, bank_s, bank_x1, bank_x2, bank_r2 = bank[0:2], bank[2:4], bank[4], [bank[5], bank[7]], bank[6]
        bank_h1, bank_l2 = [bank_x1, bank_x2[0], bank_r2, bank_a[0]], bank_a[1]

        idx_in, w1_in, w0_in, w0b_in, w2_in = (sem(n) for n in ("idx_in", "w1_in", "w0_in", "w0b_in", "w2_in"))
        const_in, early_in, context_in, wt1_in, wt2_in, y_out = (
            sem(n) for n in ("const_in", "early_in", "context_in", "wt1_in", "wt2_in", "y_out"))
        gathered0_early = sem("gathered0_early")
        gathered = [sem("gathered0"), sem("gathered1")] + [sem("gathered_later")] * (BLOCKS - 2)
        w1_high_ready, w1_low_ready, w0_summed, w0_ready, w0_high_ready, w0_low_ready, bias_ready, sel_ready = (
            sem(n) for n in ("w1_high_ready", "w1_low_ready", "w0_summed", "w0_ready", "w0_high_ready",
                             "w0_low_ready", "bias_ready", "sel_ready"))
        taken_off = sem("taken_off")
        high_ready = sem("high_ready")
        rest_ready = sem("rest_ready")
        mid_ready = sem("mid_ready")
        low_ready = sem("low_ready")
        eye_ready = sem("eye_ready")
        turned = sem("turned")
        parts_ready = sem("parts_ready")
        l0_selected = sem("l0_selected")
        z0_ready = sem("z0_ready")
        z0_high_ready = sem("z0_high_ready")
        z0_low_ready = sem("z0_low_ready")
        l0_high_done = sem("l0_high_done")
        l0_done = sem("l0_done")
        x1_ready = sem("x1_ready")
        x1_spread = [sem(f"x1_spread{i}") for i in range(A_PAIRS)]
        x1_pooled = sem("x1_pooled")
        a_ready = sem("a_ready")
        z_ready = sem("z_ready")
        z_high_ready = sem("z_high_ready")
        z_low_dve = sem("z_low_dve")
        z_low_pool = sem("z_low_pool")
        used = sem("used")
        x2_ready = sem("x2_ready")
        x2_pooled = sem("x2_pooled")
        x0_turned = sem("x0_turned")
        x2_turned = sem("x2_turned")
        diag_ready = sem("diag_ready")
        x2T_ready = sem("x2T_ready")
        g_done = sem("g_done")
        g_ready = sem("g_ready")
        l2_done = sem("l2_done")
        res2_ready = sem("res2_ready")
        dense_ready = sem("dense_ready")
        h1_done, h1_ready, h2_done, h2_ready, y_done, y_ready = (
            sem(n) for n in ("h1_done", "h1_ready", "h2_done", "h2_ready", "y_done", "y_ready"))

        def wait(eng, semaphore, value):
            if not isinstance(value, int) or value > 0:
                eng.wait_ge(semaphore, value)

        def part_wait(eng):
            eng.wait_ge(const_in, CONSTANTS * DMA_INC)

        def taker(blk, q, i):
            return takers(PER_BLOCK * (blk if isinstance(blk, int) else 1) + q)[i]

        def low_count(who, blk, q, i):
            if not isinstance(blk, int):
                per_block = low_count(who, 2, 0, -1) - low_count(who, 1, 0, -1)
                return (blk - 1) * per_block + low_count_in(who, 1, q, i)
            return low_count_in(who, blk, q, i)

        def low_count_in(who, blk, q, i):
            n = 0
            for step in range(PER_BLOCK * blk + q + 1):
                kinds = takers(step)
                n += sum(k == who for k in (kinds if step < PER_BLOCK * blk + q else kinds[:i + 1]))
            return n

        def before(blk, q, i, back):
            i -= back
            if i < 0:
                i, q = i + PAIRS, q - 1
            if q < 0:
                if isinstance(blk, int) and blk == 0:
                    return None
                q += PER_BLOCK
                blk = blk - 1
            return blk, q, i

        def wait_low(eng, blk, q, i):
            who = taker(blk, q, i)
            eng.wait_ge(z_low_pool if who == "pool" else z_low_dve, low_count(who, blk, q, i))

        def splits(blk):
            return blk + 2

        def is_last(blk):
            return isinstance(blk, int) and blk == BLOCKS - 1

        def turns(blk, q):
            return [] if is_last(blk) else [(at, m, 4 * (blk + 1) + m) for at, m in TURNS.get(q, [])]

        def has_next(blk, q):
            return not (isinstance(blk, int) and PER_BLOCK * blk + q == STEPS - 1)

        def is_step(blk, q, n):
            return isinstance(blk, int) and PER_BLOCK * blk + q == n

        def parity(blk):
            return blk % 2 if isinstance(blk, int) else blk * (-1) + 2

        def tile_columns(blk, q, at=0, size=TILE):
            half = parity(blk)
            if q < 0 or q >= PER_BLOCK:
                half = (1 - half) if isinstance(blk, int) else blk - 1
            return parts[:, bass.ds(half * (P * DIM) + (q % PER_BLOCK) * TILE + at, size)]

        def next_block_columns(blk, quarter):
            half = (1 - parity(blk)) if isinstance(blk, int) else blk - 1
            cols = parts[:, bass.ds(half * (P * DIM), P * DIM)].rearrange("p (b d) -> p b d", d=DIM)
            return cols[:, :, QUART * quarter:QUART * (quarter + 1)]

        def rows_by_dim(rows):
            return rows.rearrange("p (f d) -> p d f", d=DIM)

        def rows_after(blk):
            return emb[:].rearrange("p a b -> p (a b)")[:, bass.ds((blk - 1) * (FIELDS * DIM), FIELDS * DIM)]

        first_rows = rows_by_dim(emb[:, 0, :])
        first_batches = [(slice(0, EARLY_FIELDS), gathered0_early), (slice(EARLY_FIELDS, FIELDS), gathered[0])]

        block = ctx.enter_context(nc.Block())

        @block.sync
        def _(sp):
            sp.dma_start(idx[:], ids).then_inc(idx_in, DMA_INC)
            for dst, src in ((eye_sb[:], eye), (sel_stage, selections),
                             (setup_flat[:, SEL_COLUMNS:sel_end], members), (mask_sb[:], mask),
                             (bias_sb[:, 0:3], bias), (bt1_sb[:], bt1), (bt2_sb[:], bt2), (wt3_sb[:], wt3)):
                sp.dma_start(dst, src).then_inc(const_in, DMA_INC)
            sp.dma_start(w1_stage, w1).then_inc(w1_in, DMA_INC)
            sp.dma_start(w0_stage, w0a).then_inc(w0_in, DMA_INC)
            sp.dma_start(w0b_stage, w0b).then_inc(w0b_in, DMA_INC)
            sp.dma_start(w2_sb[:], w2).then_inc(w2_in, DMA_INC)

            def spread_x1(t):
                if isinstance(t, int) and t == 0:
                    sp.wait_ge(x1_ready, 1)
                for pair in range(A_PAIRS):
                    wait(sp, z_ready, PAIRS * (t - 1) + PAIRS - A_PAIRS + pair + 1 if has_tile_before(t) else 0)
                    for b in (2 * pair, 2 * pair + 1):
                        rows = x1[K_GROUP * b:K_GROUP * (b + 1), :]
                        sp.dma_start(x1_rep[:, b, :], rows.unsqueeze(1).to_broadcast([K_GROUP, J_GROUP, TILE])
                                     ).then_inc(x1_spread[pair], DMA_INC)

            def has_tile_before(t):
                return not (isinstance(t, int) and t == 0)

            def steps(blk):
                for q in range(PER_BLOCK):
                    if has_next(blk, q):
                        spread_x1(PER_BLOCK * blk + q + 1)

            spread_x1(0)
            steps(0)
            with sp.Fori(1, BLOCKS - 1) as blk:
                steps(blk)
            sp.wait_ge(parts_ready, 4 * BLOCKS)
            sp.dma_start(wt1_early, wt1[0:P, :]).then_inc(early_in, DMA_INC)
            sp.dma_start(context_w_stage, wt1_dense).then_inc(context_in, DMA_INC)
            sp.dma_start(context_stage, dense).then_inc(context_in, DMA_INC)
            steps(BLOCKS - 1)
            sp.wait_ge(z_ready, PAIRS * STEPS)
            sp.dma_start(wt1_sb, wt1[P:3 * P, :].rearrange("(c p) n -> p c n", p=P)).then_inc(wt1_in, DMA_INC)
            sp.dma_start(wt2_sb, wt2.rearrange("(c p) n -> p c n", p=P)).then_inc(wt2_in, DMA_INC)
            sp.wait_ge(y_ready, 1)
            sp.dma_start(out.rearrange("b o -> o b"), y_sb).then_inc(y_out, DMA_INC)
            sp.wait_ge(y_out, DMA_INC)

        @block.gpsimd
        def _(pool):
            def gather(blk, f):
                pool.indirect_dma_start(emb[:, blk % 2, f * DIM:(f + 1) * DIM], None, tables[f],
                                        bass.IndirectOffsetOnAxis(ap=idx[:, blk, f:f + 1], axis=0)
                                        ).then_inc(gathered0_early if blk == 0 and f < EARLY_FIELDS else gathered[blk],
                                                   DMA_INC)

            def gather_next():
                blk, f = todo.pop(0)
                if f == 0 and blk >= 2:
                    pool.wait_ge(rest_ready, splits(blk - 2))
                    wait(pool, gathered[blk], (blk - 2) * FIELDS * DMA_INC)
                gather(blk, f)

            pool.wait_ge(idx_in, DMA_INC)
            for f in range(FIELDS):
                gather(0, f)
            todo = [(b, f) for b in range(1, BLOCKS) for f in range(FIELDS)]
            for _ in range(GATHERS_BEFORE):
                gather_next()
            for step in range(STEPS):
                blk, q = divmod(step, PER_BLOCK)
                for i in range(PAIRS):
                    if taker(blk, q, i) == "pool":
                        pool.wait_ge(z_high_ready, PAIRS * step + i + 1)
                        wait(pool, used, PAIRS * step + i + 1 - RING_LOW)
                        pool.tensor_tensor(Z_low[:, i % RING_LOW, :], Z[:, i % RING, :],
                                           Z_high[:, i % RING, :].bitcast(F32), ALU.subtract).then_inc(z_low_pool, 1)
                    n = GATHERS[step]
                    if (i + 1) * n // PAIRS > i * n // PAIRS:
                        gather_next()

        @block.scalar
        def _(act):
            def copy(dst, src):
                return nc.scalar.copy(dst, src)

            def keep_quarter(blk, m, number, src):
                part_wait(act)
                act.wait_ge(turned, number + 1)
                if m == 0 and not (isinstance(blk, int) and blk <= 0):
                    act.wait_ge(x0_turned, PER_BLOCK * blk)
                copy(next_block_columns(blk, m), src[0:STACK, :].rearrange("p (d b) -> p b d", d=QUART)
                     ).then_inc(parts_ready, 1)

            def square(t, k, rest_read=None):
                z = z0[k % 2]
                if k == 0:
                    wait(act, g_done, SUB * (t - 2))
                if k == 1 and rest_read is not None:
                    act.wait_ge(low_ready, rest_read)
                act.wait_ge(l0_selected, L0_TILES * t + k + 1)
                wait(act, z0_low_ready, L0_TILES * t + max(k - 1, 0))
                nc.scalar.activation(z, bank_s[k % 2][:], ACT.Square).then_inc(z0_ready, 1)

            def square_high(t, k):
                act.wait_ge(z0_ready, L0_TILES * t + k + 1)
                if k < 2:
                    wait(act, l0_done, L0_TILES * t)
                else:
                    act.wait_ge(l0_high_done, LAST * t + k - 1)
                copy(z0_high[:, k % 2, :], z0[k % 2]).then_inc(z0_high_ready, 1)

            def evacuate_x1(t):
                act.wait_ge(l0_done, L0_TILES * (t + 1))
                wait(act, x1_pooled, t)
                nc.scalar.activation(x1[:], bank_x1[:], ACT.Identity, bias=bias_sb[:, 0:1]).then_inc(x1_ready, 1)

            def diagonal(n):
                act.wait_ge(x0_turned, n)
                wait(act, g_done, SUB * (n - 1))
                x0_cols = bank_s[0][:, 0:SUB * FIELDS].rearrange("p (s j) -> p s j", j=FIELDS)
                for b in range(SUB_ROWS):
                    last = nc.scalar.activation(x0_diag[:, :, b, 0:FIELDS], x0_cols, ACT.Copy, scale=mask_sb[:, b:b + 1])
                last.then_inc(diag_ready, 1)

            def evacuate_x2(n, q):
                act.wait_ge(used, PAIRS * n)
                wait(act, x2_turned, n - 1)
                nc.scalar.activation(x2[:], bank_x2[q % 2][:], ACT.Identity,
                                     bias=bias_sb[:, 1:2]).then_inc(x2_ready, 1)

            def evacuate_x2T(n, squares_done):
                act.wait_ge(x2_turned, n)
                wait(act, g_done, SUB * (n - 1))
                wait(act, z0_low_ready, squares_done)
                copy(x2T[:].rearrange("p a b -> p (a b)"), bank_s[1][:]).then_inc(x2T_ready, 1)

            def evacuate_g(n, tile, sub, blocks_done):
                act.wait_ge(g_done, SUB * (n - 1) + sub + 1)
                if tile == 0 and sub == 0:
                    wait(act, l2_done, blocks_done)
                    wait(act, x2_pooled, blocks_done)
                at = ROWS * tile + SUB_ROWS * sub
                copy(G[:, :, at:at + SUB_ROWS].rearrange("p j b -> p b j"),
                     bank_s[sub % 2][:, 0:SUB_ROWS * G_COLUMNS].rearrange("p (b j) -> p b j", j=G_COLUMNS)
                     ).then_inc(g_ready, 1)

            def keep_pooled_x2(number):
                part_wait(act)
                act.wait_ge(g_ready, PER_BLOCK * SUB * (number + 1))
                copy(res[:, 1, bass.ds(number * P, P)], G[:, FIELDS, :]).then_inc(x2_pooled, 1)

            def evacuate_res2(number, src=bank_r2):
                part_wait(act)
                act.wait_ge(l2_done, number + 1)
                nc.scalar.activation(res[:, 2, bass.ds(number * L2_ROWS, L2_ROWS)], src[:, 0:L2_ROWS], ACT.Identity,
                                     bias=bias_sb[:, 3:4]).then_inc(res2_ready, 1)

            act.wait_ge(const_in, CONSTANTS * DMA_INC)
            nc.scalar.mul(bias_sb[:, 3:4], bias_sb[:, 2:3], float(DIM)).then_inc(bias_ready, 1)
            copy(sel_sb[:], sel_stage).then_inc(sel_ready, 1)
            copy(x0_diag[:, :, :, FIELDS], mask_sb[:].unsqueeze(1).to_broadcast([P, SUB, SUB_ROWS]))
            act.wait_ge(w1_in, DMA_INC)
            copy(w1_high[:].rearrange("p t h -> p (t h)"), w1_stage).then_inc(w1_high_ready, 1)
            act.wait_ge(w0_ready, 1)
            copy(w0_high[:].rearrange("p t h -> p (t h)"), w0_stage).then_inc(w0_high_ready, 1)
            copy(eye_bf[:], eye_sb[:]).then_inc(eye_ready, 1)
            for n, (fields, done) in enumerate(first_batches):
                act.wait_ge(done, (fields.stop - fields.start) * DMA_INC)
                copy(split[:, :, 0, fields], first_rows[:, :, fields]).then_inc(high_ready, 1)
                act.wait_ge(rest_ready, n + 1)
                copy(split[:, :, 1, fields], rest[:, :, fields]).then_inc(mid_ready, 1)
            for m in (0, 2):
                keep_quarter(-1, m, m, bank[m])
            for k in range(L0_TILES):
                square(0, k, 2)
                square_high(0, k)
            evacuate_x1(0)
            act.wait_ge(bias_ready, 1)

            def steps(blk, next_rows=None, next_gathered=None, next_count=None):
                for q in range(PER_BLOCK):
                    n = PER_BLOCK * blk + q
                    t = n + 1
                    todo = turns(blk, q)
                    for i in range(PAIRS):
                        if i == 4 and not is_step(blk, q, 0):
                            evacuate_x2(n, q - 1)
                        if has_next(blk, q) and 4 <= i < 4 + L0_TILES:
                            square(t, i - 4, splits(blk) + 1 if q == SPLIT_STEP + 1 and not is_last(blk) else None)
                        if i == 13 and has_next(blk, q):
                            evacuate_x1(t)
                        if q == SPLIT_STEP and not is_last(blk):
                            if i == SPLIT_AT:
                                part_wait(act)
                                act.wait_ge(next_gathered, next_count)
                                wait(act, turned, 4 * (blk + 1))
                                copy(split[:, :, 0, :], rows_by_dim(next_rows)).then_inc(high_ready, 1)
                            if i == SPLIT_AT + 4:
                                act.wait_ge(rest_ready, splits(blk) + 1)
                                copy(split[:, :, 1, :], rest).then_inc(mid_ready, 1)
                        for at, m, number in todo:
                            if i == at + TURN_LAG:
                                keep_quarter(blk, m, number, bank_x2[(q - 1) % 2])
                        if not is_step(blk, q, 0):
                            if i == 13:
                                diagonal(n)
                                evacuate_x2T(n, L0_TILES * (t + 1 if has_next(blk, q) else STEPS))
                            if q == 1 and not is_step(blk, q, 1):
                                if i == 14:
                                    keep_pooled_x2(blk - 1)
                                if i == 16:
                                    evacuate_res2(blk - 1)
                            if i >= 16:
                                evacuate_g(n, (q - 1) % PER_BLOCK, i - 16, blk)
                        act.wait_ge(z_ready, PAIRS * n + i + 1)
                        wait(act, used, PAIRS * n + i + 1 - RING)
                        copy(Z_high[:, i % RING, :], Z[:, i % RING, :]).then_inc(z_high_ready, 1)
                        if has_next(blk, q) and 4 <= i < 4 + L0_TILES:
                            square_high(t, i - 4)

            steps(0, emb[:, 1, :], gathered[1], FIELDS * DMA_INC)
            with act.Fori(1, BLOCKS - 1) as blk:
                steps(blk, rows_after(blk), gathered[2], blk * (FIELDS * DMA_INC))
            steps(BLOCKS - 1)

            n = STEPS
            evacuate_x2(n, n - 1)
            diagonal(n)
            evacuate_x2T(n, L0_TILES * STEPS)
            for sub in range(SUB):
                evacuate_g(n, PER_BLOCK - 1, sub, 0)
            keep_pooled_x2(BLOCKS - 1)
            evacuate_res2(BLOCKS - 1, bank_l2)
            for m in range(TOP1 // P):
                act.wait_ge(h1_done, m + 1)
                nc.scalar.activation(h1[:, m, :], bank_h1[m][:], ACT.Relu, bias=bt1_sb[:, m:m + 1]).then_inc(h1_ready, 1)
            for m in range(TOP2 // P):
                act.wait_ge(h2_done, m + 1)
                nc.scalar.activation(h2[:, m, :], bank_s[m][:], ACT.Relu, bias=bt2_sb[:, m:m + 1]).then_inc(h2_ready, 1)
            act.wait_ge(y_done, 1)
            copy(y_sb, bank_l2[0:1, :]).then_inc(y_ready, 1)

        @block.vector
        def _(dve):
            def l0_low(t, k):
                dve.wait_ge(z0_high_ready, L0_TILES * t + k + 1)
                if k < LAST:
                    wait(dve, l0_done, L0_TILES * t + max(k - 1, 0))
                    nc.vector.tensor_tensor(z0_low[:, k % 2, :], z0[k % 2], z0_high[:, k % 2, :].bitcast(F32),
                                            ALU.subtract).then_inc(z0_low_ready, 1)
                else:
                    third = slice(2 * LAST_ROWS, 3 * LAST_ROWS)
                    high = z0_high[third, k % 2, :]
                    nc.vector.tensor_tensor(high, z0[k % 2][third, :], high.bitcast(F32),
                                            ALU.subtract).then_inc(z0_low_ready, 1)

            def pool_x1(t):
                part_wait(dve)
                dve.wait_ge(x1_ready, t + 1)
                nc.vector.reduce_sum(res[:, 0, bass.ds(t * ROWS, ROWS)],
                                     x1[:].rearrange("p (b d) -> p b d", d=DIM), AX.X).then_inc(x1_pooled, 1)

            def low_part(at):
                blk, q, i = at
                n = PER_BLOCK * blk + q
                dve.wait_ge(z_high_ready, PAIRS * n + i + 1)
                wait(dve, used, PAIRS * n + i + 1 - RING_LOW)
                nc.vector.tensor_tensor(Z_low[:, i % RING_LOW, :], Z[:, i % RING, :], Z_high[:, i % RING, :].bitcast(F32),
                                        ALU.subtract).then_inc(z_low_dve, 1)

            dve.wait_ge(w0_in, DMA_INC)
            dve.wait_ge(w0b_in, DMA_INC)
            nc.vector.tensor_tensor(w0_stage, w0_stage, w0b_stage, ALU.add).then_inc(w0_summed, 1)
            dve.wait_ge(w0_summed, 1)
            nc.vector.tensor_scalar(w0_stage, w0_stage, 0.5, None, ALU.mult).then_inc(w0_summed, 1)
            dve.wait_ge(taken_off, 1)
            squares = w0_stage[0:FIELDS, SQUARES * HID:(SQUARES + 1) * HID]
            nc.vector.tensor_tensor(squares, squares, bank_x1[0:FIELDS, 0:HID], ALU.subtract).then_inc(w0_ready, 1)
            dve.wait_ge(w0_high_ready, 1)
            nc.vector.tensor_tensor(w0_low[:].rearrange("p t h -> p (t h)"), w0_stage,
                                    w0_high[:].rearrange("p t h -> p (t h)").bitcast(F32), ALU.subtract).then_inc(w0_low_ready, 1)
            dve.wait_ge(w0_low_ready, 1)
            second = slice(LAST_ROWS, 2 * LAST_ROWS)
            nc.vector.tensor_copy(w0_high[second, LAST, :], w0_low[second, LAST, :].bitcast(F32)).then_inc(w0_low_ready, 1)
            dve.wait_ge(w1_high_ready, 1)
            nc.vector.tensor_tensor(w1_low[:].rearrange("p t h -> p (t h)"), w1_stage,
                                    w1_high[:].rearrange("p t h -> p (t h)").bitcast(F32), ALU.subtract).then_inc(w1_low_ready, 1)
            for n, (fields, done) in enumerate(first_batches):
                dve.wait_ge(done, (fields.stop - fields.start) * DMA_INC)
                dve.wait_ge(high_ready, n + 1)
                nc.vector.tensor_tensor(rest[:, :, fields], first_rows[:, :, fields], split[:, :, 0, fields],
                                        ALU.subtract).then_inc(rest_ready, 1)
                dve.wait_ge(mid_ready, n + 1)
                nc.vector.tensor_tensor(split[:, :, 2, fields], rest[:, :, fields], split[:, :, 1, fields],
                                        ALU.subtract).then_inc(low_ready, 1)
            for m in (1, 3):
                dve.wait_ge(turned, m + 1)
                nc.vector.tensor_copy(next_block_columns(-1, m), bank[m][0:STACK, :].rearrange("p (d b) -> p b d", d=QUART)
                                      ).then_inc(parts_ready, 1)
            dve.wait_ge(const_in, CONSTANTS * DMA_INC)
            for k in range(L0_TILES):
                l0_low(0, k)
            pool_x1(0)

            def steps(blk, next_rows=None, next_gathered=None, next_count=None):
                for q in range(PER_BLOCK):
                    n = PER_BLOCK * blk + q
                    t = n + 1
                    for i in range(PAIRS):
                        if has_next(blk, q):
                            if 6 <= i < 6 + L0_TILES:
                                l0_low(t, i - 6)
                            if i == 15:
                                pool_x1(t)
                        if q == SPLIT_STEP and not is_last(blk):
                            if i == SPLIT_AT + 3:
                                dve.wait_ge(next_gathered, next_count)
                                dve.wait_ge(high_ready, splits(blk) + 1)
                                dve.wait_ge(z0_low_ready, L0_TILES * t + LAST)
                                nc.vector.tensor_tensor(rest, rows_by_dim(next_rows), split[:, :, 0, :],
                                                        ALU.subtract).then_inc(rest_ready, 1)
                            if i == SPLIT_AT + 6:
                                dve.wait_ge(mid_ready, splits(blk) + 1)
                                nc.vector.tensor_tensor(split[:, :, 2, :], rest, split[:, :, 1, :],
                                                        ALU.subtract).then_inc(low_ready, 1)
                        if not has_next(blk, q) and i == 3:
                            second, third = (slice(n * LAST_ROWS, (n + 1) * LAST_ROWS) for n in (1, 2))
                            dve.wait_ge(context_in, 2 * DMA_INC)
                            dve.wait_ge(l0_done, L0_TILES * STEPS)
                            nc.vector.tensor_copy(context, context_stage).then_inc(dense_ready, 1)
                            nc.vector.tensor_copy(context_w, context_w_stage).then_inc(dense_ready, 1)
                            for part, whole, at in ((context, context_stage, third), (context_w, context_w_stage, second)):
                                dve.wait_ge(dense_ready, 2)
                                nc.vector.tensor_tensor(part[at], whole[at], part[at].bitcast(F32),
                                                        ALU.subtract).then_inc(dense_ready, 1)
                        a, b = i // A_PAIRS, 2 * (i % A_PAIRS)
                        if i % A_PAIRS == 0:
                            dve.wait_ge(a_ready, A_GROUPS * n + a + 1)
                        if i < A_PAIRS:
                            dve.wait_ge(x1_spread[i], 2 * DMA_INC * (n + 1))
                        last_user = before(blk, q, i, RING)
                        if last_user is not None:
                            wait_low(dve, *last_user)
                        nc.vector.tensor_tensor(
                            Z[:, i % RING, :].rearrange("p (u c) -> p u c", u=2),
                            bank_a[(q + a) % 2][:].unsqueeze(1).to_broadcast([P, 2, TILE]),
                            x1_rep[:, b:b + 2, :], ALU.mult).then_inc(z_ready, 1)
                        due = before(blk, q, i, LOW_LAG)
                        if due is not None and taker(*due) == "dve":
                            low_part(due)

            steps(0, emb[:, 1, :], gathered[1], FIELDS * DMA_INC)
            with dve.Fori(1, BLOCKS - 1) as blk:
                steps(blk, rows_after(blk), gathered[2], blk * (FIELDS * DMA_INC))
            steps(BLOCKS - 1)
            for i in range(PAIRS - LOW_LAG, PAIRS):
                if taker(BLOCKS - 1, PER_BLOCK - 1, i) == "dve":
                    low_part((BLOCKS - 1, PER_BLOCK - 1, i))

        @block.tensor
        def _(pe):
            mm = nc.tensor.matmul

            def turn_quarter(m, dst):
                for d in range(QUART):
                    last = mm(dst[0:STACK, P * d:P * (d + 1)], split[:, QUART * m + d].rearrange("p a f -> p (a f)"),
                              eye_bf[:], start=True, stop=True)
                last.then_inc(turned, 1)

            def keep_clock(count):
                for _ in range(count):
                    mm(bank_r2[:], sel_sb[:, SEL0:SEL0 + P], sel_sb[:, 0:TILE], start=True, stop=True)

            def l0_select(blk, q, k):
                mm(bank_s[k % 2][:], sel0_sb[:, k, :], tile_columns(blk, q),
                   start=True, stop=True).then_inc(l0_selected, 1)

            def l0_high(t, k):
                if k == 0:
                    wait(pe, x1_ready, t)
                pe.wait_ge(z0_high_ready, L0_TILES * t + k + 1)
                mm(bank_x1[:], w0_low[:, k, :], z0_high[:, k % 2, :], start=(k == 0), stop=False)
                mm(bank_x1[:], w0_high[:, k, :], z0_high[:, k % 2, :],
                   start=False, stop=False).then_inc(l0_high_done, 1)

            def l0_low(t, k):
                pe.wait_ge(z0_low_ready, L0_TILES * t + k + 1)
                if k < LAST:
                    mm(bank_x1[:], w0_high[:, k, :], z0_low[:, k % 2, :], start=False, stop=False).then_inc(l0_done, 1)
                else:
                    mm(bank_x1[:], w0_high[0:3 * LAST_ROWS, k, :], z0_high[0:3 * LAST_ROWS, k % 2, :],
                       start=False, stop=True).then_inc(l0_done, 1)

            def select_fields(blk, q, a):
                mm(bank_a[(q + a) % 2][:], selA_sb[:, a, :], tile_columns(blk, q),
                   start=True, stop=True).then_inc(a_ready, 1)

            def high_products(n, q, i):
                pe.wait_ge(z_high_ready, PAIRS * n + i + 1)
                for u in range(2):
                    for w in (w1_high, w1_low):
                        mm(bank_x2[q % 2][:], w[:, 2 * i + u, :], Z_high[:, i % RING, u * TILE:(u + 1) * TILE],
                           start=(i == 0 and u == 0 and w is w1_high), stop=False)

            def low_products(at):
                blk, q, i = at
                wait_low(pe, blk, q, i)
                for u in range(2):
                    last = mm(bank_x2[q % 2][:], w1_high[:, 2 * i + u, :], Z_low[:, i % RING_LOW, u * TILE:(u + 1) * TILE],
                              start=False, stop=(i == PAIRS - 1 and u == 1))
                last.then_inc(used, 1)

            def turn_x0(blk, q):
                for s in range(SUB):
                    last = mm(bank_s[0][:, s * FIELDS:(s + 1) * FIELDS], tile_columns(blk, q - 1, s * P, P),
                              selT_sb[:], start=True, stop=True)
                last.then_inc(x0_turned, 1)

            def turn_x2(n):
                pe.wait_ge(x2_ready, n)
                for s in range(SUB):
                    last = nc.tensor.transpose(bank_s[1][:, s * P:(s + 1) * P], x2[:, s * P:(s + 1) * P], eye_sb[:])
                last.then_inc(x2_turned, 1)

            def g_product(n, sub):
                if sub == 0:
                    pe.wait_ge(diag_ready, n)
                    pe.wait_ge(x2T_ready, n)
                if sub >= 2:
                    pe.wait_ge(g_ready, SUB * (n - 1) + sub - 1)
                mm(bank_s[sub % 2][:, 0:SUB_ROWS * G_COLUMNS], x2T[:, sub, :],
                   x0_diag[:, sub].rearrange("p b j -> p (b j)"), start=True, stop=True).then_inc(g_done, 1)

            def l2_product(number, j, dst=bank_r2):
                if j == 0:
                    pe.wait_ge(g_ready, PER_BLOCK * SUB * (number + 1))
                    wait(pe, res2_ready, number)
                last = mm(dst[:, 0:L2_ROWS], w2_sb[:, j, :], G[:, j, :], start=(j == 0), stop=(j == FIELDS - 1))
                if j == FIELDS - 1:
                    last.then_inc(l2_done, 1)

            pe.wait_ge(const_in, CONSTANTS * DMA_INC)
            pe.wait_ge(w0_summed, 2)
            for k in range(L0_TILES):
                last = mm(bank_x1[0:FIELDS, 0:HID], members_sb[:, k, :], w0_stage[:, k * HID:(k + 1) * HID],
                          start=(k == 0), stop=(k == L0_TILES - 1))
            last.then_inc(taken_off, 1)
            pe.wait_ge(sel_ready, 1)
            pe.wait_ge(gathered0_early, EARLY_FIELDS * DMA_INC)
            keep_clock(CLOCK_BEFORE_TURNS)
            pe.wait_ge(eye_ready, 1)
            pe.wait_ge(low_ready, 2)
            for m in range(DIM // QUART):
                turn_quarter(m, bank[m])
            keep_clock(CLOCK_BEFORE_SUMS)
            pe.wait_ge(parts_ready, 4)
            pe.wait_ge(w0_low_ready, 2)
            for k in range(L0_TILES):
                if k >= 2:
                    pe.wait_ge(z0_ready, k - 1)
                l0_select(0, 0, k)
                if k == 1:
                    keep_clock(CLOCK_AT_SUMS)
                if k >= 1:
                    l0_high(0, k - 1)
                if k >= 2:
                    l0_low(0, k - 2)
            for k in range(LAST - 1, L0_TILES):
                l0_low(0, k)
            for a in range(2):
                select_fields(0, 0, a)
            pe.wait_ge(w1_low_ready, 1)
            pe.wait_ge(w2_in, DMA_INC)
            keep_clock(CLOCK_BEFORE_STEPS)

            def free_of_step_before(blk, q, b):
                n = PER_BLOCK * blk + q
                if is_step(blk, q, 0) or is_step(blk, q, 1):
                    pe.wait_ge(z0_ready, L0_TILES * (n + 1) - b)
                else:
                    pe.wait_ge(g_ready, SUB * (n - 1) - 1 + b)

            def steps(blk):
                for q in range(PER_BLOCK):
                    n = PER_BLOCK * blk + q
                    t = n + 1
                    todo = turns(blk, q)
                    for i in range(PAIRS):
                        if has_next(blk, q):
                            if i == 0:
                                if q == PER_BLOCK - 1:
                                    pe.wait_ge(parts_ready, t + 4)
                                free_of_step_before(blk, q, 0)
                                l0_select(blk, q + 1, 0)
                                free_of_step_before(blk, q, 1)
                                l0_select(blk, q + 1, 1)
                            k = i - 2
                            if 0 <= k < LAST:
                                if k + 2 < L0_TILES:
                                    pe.wait_ge(z0_ready, L0_TILES * t + k + 1)
                                    l0_select(blk, q + 1, k + 2)
                                l0_high(t, k)
                            if 1 <= k <= L0_TILES:
                                l0_low(t, k - 1)
                        for at, m, number in todo:
                            if i == at:
                                wait(pe, x2_ready, n)
                                if m == 0:
                                    pe.wait_ge(low_ready, splits(blk) + 1)
                                else:
                                    pe.wait_ge(parts_ready, number)
                                turn_quarter(m, bank_x2[(q - 1) % 2])
                        if not is_step(blk, q, 0):
                            if i == 9:
                                if has_next(blk, q):
                                    pe.wait_ge(z0_ready, L0_TILES * t + L0_TILES)
                                else:
                                    free_of_step_before(blk, q, 0)
                                turn_x0(blk, q)
                            if i == 10:
                                if has_next(blk, q):
                                    pe.wait_ge(z0_ready, L0_TILES * t + L0_TILES - 1)
                                else:
                                    free_of_step_before(blk, q, 1)
                                turn_x2(n)
                            if 13 <= i < 13 + SUB:
                                g_product(n, i - 13)
                            if q == 1 and not is_step(blk, q, 1):
                                for j in range(3 * i, min(3 * i + 3, FIELDS)):
                                    l2_product(blk - 1, j)
                        if i % A_PAIRS == FIELDS_AT:
                            a = i // A_PAIRS
                            if a + 2 < A_GROUPS or has_next(blk, q):
                                pe.wait_ge(z_ready, PAIRS * n + A_PAIRS * (a + 1))
                                if a + 2 < A_GROUPS:
                                    select_fields(blk, q, a + 2)
                                else:
                                    select_fields(blk, q + 1, a + 2 - A_GROUPS)
                        if not has_next(blk, q) and i in (12, 14, 16):
                            top1_early((i - 12) // 2)
                        if i == 0:
                            wait(pe, x2_ready, n - 1)
                            if q - 1 in TURNS and not is_last(blk):
                                wait(pe, parts_ready, 4 * (blk + 1) + TURNS[q - 1][-1][1] + 1)
                        high_products(n, q, i)
                        late = before(blk, q, i, 1)
                        if late is not None:
                            low_products(late)

            def top1(m, c, weights, of=slice(0, BATCH), start=False, stop=False):
                return mm(bank_h1[m][:, of], weights[:, m * P:(m + 1) * P], res[:, c, of], start=start, stop=stop)

            def top1_early(m):
                pe.wait_ge(early_in, DMA_INC)
                pe.wait_ge(x1_pooled, STEPS)
                top1(m, 0, wt1_early, start=True)
                pe.wait_ge(dense_ready, 4)
                mm(bank_h1[m][:], context_w[:, m * P:(m + 1) * P], context[:], start=False, stop=False)

            steps(0)
            with pe.Fori(1, BLOCKS - 1) as blk:
                steps(blk)
            steps(BLOCKS - 1)
            free_of_step_before(BLOCKS, 0, 0)
            turn_x0(BLOCKS, 0)
            low_products((BLOCKS - 1, PER_BLOCK - 1, PAIRS - 1))
            free_of_step_before(BLOCKS, 0, 1)
            pe.wait_ge(z_ready, PAIRS * STEPS)
            top1_early(3)
            turn_x2(STEPS)
            blocks_before, last_block = slice(0, BATCH - P), slice(BATCH - P, BATCH)
            pe.wait_ge(wt1_in, DMA_INC)
            pe.wait_ge(x2_pooled, BLOCKS - 1)
            for m in range(TOP1 // P):
                top1(m, 1, wt1_sb[:, 0], blocks_before)
            pe.wait_ge(res2_ready, BLOCKS - 1)
            for sub in range(SUB):
                g_product(STEPS, sub)
                top1(sub, 2, wt1_sb[:, 1], blocks_before)
            for j in range(FIELDS):
                l2_product(BLOCKS - 1, j, bank_l2)
            pe.wait_ge(x2_pooled, BLOCKS)
            for m in range(TOP1 // P):
                top1(m, 1, wt1_sb[:, 0], last_block)
            pe.wait_ge(res2_ready, BLOCKS)
            for m in range(TOP1 // P):
                top1(m, 2, wt1_sb[:, 1], last_block, stop=True).then_inc(h1_done, 1)
            pe.wait_ge(wt2_in, DMA_INC)
            for c in range(TOP1 // P):
                pe.wait_ge(h1_ready, c + 1)
                for m in range(TOP2 // P):
                    last = mm(bank_s[m][:], wt2_sb[:, c, m * P:(m + 1) * P], h1[:, c, :], start=(c == 0), stop=(c == 3))
                    if c == TOP1 // P - 1:
                        last.then_inc(h2_done, 1)
            for c in range(TOP2 // P):
                pe.wait_ge(h2_ready, c + 1)
                last = mm(bank_l2[0:1, :], wt3_sb[:, c:c + 1], h2[:, c, :], start=(c == 0), stop=(c == 1))
            last.then_inc(y_done, 1)


def layouts(v):
    f = np.arange(FIELDS)
    w0 = v["L0_rec_W0"].reshape(HID, FIELDS, FIELDS)
    w0a = np.zeros((P, L0_TILES, HID), np.float32)
    w0b = np.zeros((P, L0_TILES, HID), np.float32)
    sel0 = np.zeros((STACK, L0_TILES, P), np.float32)
    members = np.zeros((P, L0_TILES, FIELDS), np.float32)
    pairs = [(j, (j + shift) % FIELDS) for shift in range(1, FIELDS // 2 + 1) for j in range(FIELDS)]
    pairs[SQUARES * P:SQUARES * P] = [(j, j) for j in range(FIELDS)]
    for n, (j, g) in enumerate(pairs):
        tile, row = divmod(n, P)
        for at in ([row] if tile < LAST else [row, row + LAST_ROWS, row + 2 * LAST_ROWS]):
            w0a[at, tile] = w0[:, j, g]
            w0b[at, tile] = w0[:, g, j]
            for field in (j, g):
                for part in range(PARTS):
                    sel0[part * FIELDS + field, tile, at] = 1
        if j != g:
            members[row, tile, [j, g]] = 1
    selA = np.zeros((STACK, A_GROUPS, P), np.float32)
    for a in range(A_GROUPS):
        for p in range(P):
            j = J_GROUP * a + p % J_GROUP
            if j < FIELDS:
                selA[[j, j + FIELDS, j + 2 * FIELDS], a, p] = 1
    selT = np.tile(np.eye(FIELDS, dtype=np.float32), (PARTS, 1))
    w1 = np.zeros((HID, A_GROUPS * J_GROUP, HID), np.float32)
    w1[:, :FIELDS] = v["L0_rec_W1"].reshape(HID, FIELDS, HID)
    w1 = w1.reshape(HID, A_GROUPS, J_GROUP, B_GROUPS, K_GROUP).transpose(4, 2, 1, 3, 0).reshape(P, -1)
    dense = np.zeros((3 * LAST_ROWS, BATCH), np.float32)
    wt1_dense = np.zeros((3 * LAST_ROWS, TOP1), np.float32)
    for n in range(3):
        dense[n * LAST_ROWS:n * LAST_ROWS + DIM] = v["dense_ctx"].T
        wt1_dense[n * LAST_ROWS:n * LAST_ROWS + DIM] = v["W_top1"][3 * HID:]
    return {
        "ids": v["ids"].reshape(BLOCKS, P, FIELDS).transpose(1, 0, 2),
        "dense": dense,
        "w0a": w0a.reshape(P, -1),
        "w0b": w0b.reshape(P, -1),
        "w1": w1,
        "w2": v["L0_rec_W2"].reshape(HID, FIELDS, HID).transpose(2, 1, 0),
        "wt1": v["W_top1"],
        "wt1_dense": wt1_dense,
        "wt2": v["W_top2"],
        "wt3": v["W_top3"].reshape(TOP2 // P, P).T,
        "bias": np.stack([v["L0_rec_b0"], v["L0_rec_b1"], v["L0_rec_b2"]], axis=1),
        "bt1": v["b_top1"].reshape(TOP1 // P, P).T,
        "bt2": v["b_top2"].reshape(TOP2 // P, P).T,
        "selections": np.concatenate([sel0.reshape(STACK, -1), selA.reshape(STACK, -1), selT], axis=1),
        "members": members.reshape(P, -1),
        "mask": np.repeat(np.eye(SUB_ROWS, dtype=np.float32), DIM, axis=0),
        "eye": np.eye(P, dtype=np.float32),
    }


def kernel(**inputs):
    import concourse.bacc as bacc
    from concourse.bass_utils import run_bass_kernel_spmd

    v = {k: np.asarray(a) for k, a in inputs.items()}
    nc = bacc.Bacc("TRN2", target_bir_lowering=False, num_devices=1)
    arrays = {}

    def given(name, a):
        arrays[name] = np.ascontiguousarray(a)
        return nc.dram_tensor(name, a.shape, mybir.dt.from_np(a.dtype), kind="ExternalInput").ap()

    args = {k: given(f"in_{k}", a) for k, a in layouts(v).items()}
    tables = [given(f"in_tbl_{f}", v[f"tbl_{f}"]) for f in range(FIELDS)]
    out = nc.dram_tensor("out_y", (BATCH, 1), F32, kind="ExternalOutput").ap()
    build(nc, tables=tables, out=out, **args)
    return run_bass_kernel_spmd(nc, [arrays], core_ids=[0]).results[0]["out_y"]
```
